# Optimizing a Trainium2 kernel written in Bass

```python
import numpy as np
import jax
import jax.numpy as jnp

def _softmax(x, axis=-1):
    return jax.nn.softmax(x, axis=axis)

def _gelu(x):
    return jax.nn.gelu(x, approximate=True)

def _silu(x):
    return jax.nn.silu(x)

def _sigmoid(x):
    return jax.nn.sigmoid(x)

def _layernorm(x, axis=-1, eps=1e-05):
    m = jnp.mean(x, axis=axis, keepdims=True)
    v = jnp.var(x, axis=axis, keepdims=True)
    return (x - m) / jnp.sqrt(v + eps)

def _scatter_add(tgt, idx, src, axis=0):
    return tgt.at[idx].add(src)

def _segment_sum(src, seg, n):
    return jax.ops.segment_sum(src, seg, n)
kernel_name = 'mk_macaron_d2_jaxref_r8_83d8ac'

def setup_inputs(seed: int=0):
    np.random.seed(seed)
    _w = jnp.asarray

    def _L0_attn_setup():
        import jax, jax.numpy as jnp
        import numpy as np
        import math
        D_MODEL = 128
        N_HEADS = 16
        D_HEAD = D_MODEL // N_HEADS
        WINDOW = 32

        def _attention(x, Wq, bq, Wk, bk, Wv, bv, Wo, bo):
            B, T, C = x.shape
            W = min(WINDOW, T)
            scale = math.sqrt(D_HEAD)

            def proj(Wm, bm):
                return (x @ Wm.T + bm).reshape(B, T, N_HEADS, D_HEAD).transpose(0, 2, 1, 3)
            Q, K, V = (proj(Wq, bq), proj(Wk, bk), proj(Wv, bv))
            scores = jnp.einsum('bhqd,bhkd->bhqk', Q, K) / scale
            idx = jnp.arange(T)
            row = idx[:, None]
            col = idx[None, :]
            allowed = (col <= row) & (row - col < W)
            scores = jnp.where(allowed[None, None], scores, -jnp.inf)
            attn = jax.nn.softmax(scores, axis=-1)
            attn = jnp.nan_to_num(attn, nan=0.0)
            out = jnp.einsum('bhqk,bhkd->bhqd', attn, V)
            out = out.transpose(0, 2, 1, 3).reshape(B, T, C)
            return out @ Wo.T + bo
        key = jax.random.key(seed)
        ks = jax.random.split(key, 9)
        B, T = (2, 256)
        x = jax.random.normal(ks[0], (B, T, D_MODEL), dtype=jnp.float32)
        s = 1.0 / math.sqrt(D_MODEL)
        Wq = jax.random.uniform(ks[1], (D_MODEL, D_MODEL), jnp.float32, -s, s)
        bq = jax.random.uniform(ks[2], (D_MODEL,), jnp.float32, -s, s)
        Wk = jax.random.uniform(ks[3], (D_MODEL, D_MODEL), jnp.float32, -s, s)
        bk = jax.random.uniform(ks[4], (D_MODEL,), jnp.float32, -s, s)
        Wv = jax.random.uniform(ks[5], (D_MODEL, D_MODEL), jnp.float32, -s, s)
        bv = jax.random.uniform(ks[6], (D_MODEL,), jnp.float32, -s, s)
        Wo = jax.random.uniform(ks[7], (D_MODEL, D_MODEL), jnp.float32, -s, s)
        bo = jax.random.uniform(ks[8], (D_MODEL,), jnp.float32, -s, s)
        return {'x': x, 'Wq': Wq, 'bq': bq, 'Wk': Wk, 'bk': bk, 'Wv': Wv, 'bv': bv, 'Wo': Wo, 'bo': bo}
    _L0_attn_in = _L0_attn_setup()

    def _L0_ffn_setup():
        import jax, jax.numpy as jnp
        import numpy as np
        B, S, H, F, E, K = (2, 128, 128, 256, 8, 2)
        key = jax.random.key(seed)
        ks = jax.random.split(key, 5)
        scale_h = 1.0 / np.sqrt(H)
        scale_f = 1.0 / np.sqrt(F)
        return {'inputs': jax.random.normal(ks[0], (B, S, H), dtype=jnp.float32), 'router_w': jax.random.normal(ks[1], (H, E), dtype=jnp.float32) * scale_h, 'w1': jax.random.normal(ks[2], (E, H, F), dtype=jnp.float32) * scale_h, 'w3': jax.random.normal(ks[3], (E, H, F), dtype=jnp.float32) * scale_h, 'w2': jax.random.normal(ks[4], (E, F, H), dtype=jnp.float32) * scale_f}
    _L0_ffn_in = _L0_ffn_setup()

    def _L1_attn_setup():
        import jax, jax.numpy as jnp
        import numpy as np
        D = 128
        H = 16
        DH = D // H
        key = jax.random.key(seed)
        ks = jax.random.split(key, 7)
        s = 0.02
        return {'z': jax.random.normal(ks[0], (8, 128, D), dtype=jnp.float32), 'ln_w': jnp.ones((D,), dtype=jnp.float32), 'ln_b': jnp.zeros((D,), dtype=jnp.float32), 'W_qkv': jax.random.normal(ks[1], (D, 3 * D), dtype=jnp.float32) * s, 'b_qkv': jnp.zeros((3 * D,), dtype=jnp.float32), 'W_proj': jax.random.normal(ks[2], (D, D), dtype=jnp.float32) * s, 'b_proj': jnp.zeros((D,), dtype=jnp.float32)}
    _L1_attn_in = _L1_attn_setup()

    def _L1_ffn_setup():
        import jax, jax.numpy as jnp
        import numpy as np
        N_EMBED = 128
        FFN_HIDDEN = 512
        NUM_EXPERTS = 8
        TOP_K = 2
        key = jax.random.key(seed)
        ks = jax.random.split(key, 8)
        d, f, E = (N_EMBED, FFN_HIDDEN, NUM_EXPERTS)
        s_d = 1.0 / np.sqrt(d)
        s_f = 1.0 / np.sqrt(f)
        return {'x': jax.random.normal(ks[0], (2, 256, d), dtype=jnp.float32), 'Wg': jax.random.uniform(ks[1], (d, E), jnp.float32, -s_d, s_d), 'bg': jax.random.uniform(ks[2], (E,), jnp.float32, -s_d, s_d), 'W1': jax.random.uniform(ks[3], (E, d, f), jnp.float32, -s_d, s_d), 'b1': jax.random.uniform(ks[4], (E, f), jnp.float32, -s_d, s_d), 'W2': jax.random.uniform(ks[5], (E, f, d), jnp.float32, -s_f, s_f), 'b2': jax.random.uniform(ks[6], (E, d), jnp.float32, -s_f, s_f)}
    _L1_ffn_in = _L1_ffn_setup()
    _d = {'L0_attn_x': _L0_attn_in['x'], 'L0_attn_Wq': _L0_attn_in['Wq'], 'L0_attn_bq': _L0_attn_in['bq'], 'L0_attn_Wk': _L0_attn_in['Wk'], 'L0_attn_bk': _L0_attn_in['bk'], 'L0_attn_Wv': _L0_attn_in['Wv'], 'L0_attn_bv': _L0_attn_in['bv'], 'L0_attn_Wo': _L0_attn_in['Wo'], 'L0_attn_bo': _L0_attn_in['bo'], 'L0_ffn_router_w': _L0_ffn_in['router_w'], 'L0_ffn_w1': _L0_ffn_in['w1'], 'L0_ffn_w3': _L0_ffn_in['w3'], 'L0_ffn_w2': _L0_ffn_in['w2'], 'L1_attn_ln_w': _L1_attn_in['ln_w'], 'L1_attn_ln_b': _L1_attn_in['ln_b'], 'L1_attn_W_qkv': _L1_attn_in['W_qkv'], 'L1_attn_b_qkv': _L1_attn_in['b_qkv'], 'L1_attn_W_proj': _L1_attn_in['W_proj'], 'L1_attn_b_proj': _L1_attn_in['b_proj'], 'L1_ffn_Wg': _L1_ffn_in['Wg'], 'L1_ffn_bg': _L1_ffn_in['bg'], 'L1_ffn_W1': _L1_ffn_in['W1'], 'L1_ffn_b1': _L1_ffn_in['b1'], 'L1_ffn_W2': _L1_ffn_in['W2'], 'L1_ffn_b2': _L1_ffn_in['b2']}
    _x0 = _d['L0_attn_x']
    _d['L0_attn_x'] = jax.random.normal(jax.random.fold_in(jax.random.key(seed), 1), (16, 512, 128), dtype=_x0.dtype)
    del _x0
    return _d

def reference(L0_attn_x, L0_attn_Wq, L0_attn_bq, L0_attn_Wk, L0_attn_bk, L0_attn_Wv, L0_attn_bv, L0_attn_Wo, L0_attn_bo, L0_ffn_router_w, L0_ffn_w1, L0_ffn_w3, L0_ffn_w2, L1_attn_ln_w, L1_attn_ln_b, L1_attn_W_qkv, L1_attn_b_qkv, L1_attn_W_proj, L1_attn_b_proj, L1_ffn_Wg, L1_ffn_bg, L1_ffn_W1, L1_ffn_b1, L1_ffn_W2, L1_ffn_b2):

    def _L0_attn_ref(x, Wq, bq, Wk, bk, Wv, bv, Wo, bo):
        import jax, jax.numpy as jnp
        import numpy as np
        import math
        D_MODEL = 128
        N_HEADS = 16
        D_HEAD = D_MODEL // N_HEADS
        WINDOW = 32

        def _attention(x, Wq, bq, Wk, bk, Wv, bv, Wo, bo):
            B, T, C = x.shape
            W = min(WINDOW, T)
            scale = math.sqrt(D_HEAD)

            def proj(Wm, bm):
                return (x @ Wm.T + bm).reshape(B, T, N_HEADS, D_HEAD).transpose(0, 2, 1, 3)
            Q, K, V = (proj(Wq, bq), proj(Wk, bk), proj(Wv, bv))
            scores = jnp.einsum('bhqd,bhkd->bhqk', Q, K) / scale
            idx = jnp.arange(T)
            row = idx[:, None]
            col = idx[None, :]
            allowed = (col <= row) & (row - col < W)
            scores = jnp.where(allowed[None, None], scores, -jnp.inf)
            attn = jax.nn.softmax(scores, axis=-1)
            attn = jnp.nan_to_num(attn, nan=0.0)
            out = jnp.einsum('bhqk,bhkd->bhqd', attn, V)
            out = out.transpose(0, 2, 1, 3).reshape(B, T, C)
            return out @ Wo.T + bo
        return _attention(x, Wq, bq, Wk, bk, Wv, bv, Wo, bo)

    def _L0_ffn_ref(inputs, router_w, w1, w3, w2):
        import jax, jax.numpy as jnp
        import numpy as np
        B, S, H, F, E, K = (2, 128, 128, 256, 8, 2)
        b, s, h = inputs.shape
        x = inputs.reshape(-1, h)
        logits = x @ router_w
        top_vals, top_idx = jax.lax.top_k(logits, K)
        importance = jax.nn.softmax(top_vals.astype(jnp.float32), axis=-1).astype(x.dtype)
        one_hot = top_idx[..., None] == jnp.arange(E)[None, None, :]
        combine = jnp.sum(jnp.where(one_hot, importance[..., None], 0.0), axis=1)
        gate = jax.nn.silu(jnp.einsum('th,ehf->etf', x, w1))
        up = jnp.einsum('th,ehf->etf', x, w3)
        expert_out = jnp.einsum('etf,efh->eth', gate * up, w2)
        out = jnp.einsum('te,eth->th', combine, expert_out)
        return out.reshape(b, s, h)

    def _L1_attn_ref(z, ln_w, ln_b, W_qkv, b_qkv, W_proj, b_proj):
        import jax, jax.numpy as jnp
        import numpy as np
        D = 128
        H = 16
        DH = D // H
        b, n, d = z.shape
        mu = jnp.mean(z, axis=-1, keepdims=True)
        var = jnp.var(z, axis=-1, keepdims=True)
        zn = (z - mu) / jnp.sqrt(var + 1e-05) * ln_w + ln_b
        qkv = (zn @ W_qkv + b_qkv).reshape(b, n, 3, H, DH)
        q = qkv[:, :, 0].transpose(0, 2, 1, 3)
        k = qkv[:, :, 1].transpose(0, 2, 1, 3)
        v = qkv[:, :, 2].transpose(0, 2, 1, 3)
        scale = 1.0 / jnp.sqrt(jnp.asarray(DH, dtype=z.dtype))
        scores = jnp.einsum('bhqd,bhkd->bhqk', q, k) * scale
        attn = jax.nn.softmax(scores, axis=-1)
        msa = jnp.einsum('bhqk,bhkd->bhqd', attn, v)
        msa_cat = msa.transpose(0, 2, 1, 3).reshape(b, n, d)
        out = msa_cat @ W_proj + b_proj
        return z + out

    def _L1_ffn_ref(x, Wg, bg, W1, b1, W2, b2):
        import jax, jax.numpy as jnp
        import numpy as np
        N_EMBED = 128
        FFN_HIDDEN = 512
        NUM_EXPERTS = 8
        TOP_K = 2
        gate_scores = jax.nn.softmax(x @ Wg + bg, axis=-1)
        topk_scores, topk_idx = jax.lax.top_k(gate_scores, TOP_K)
        topk_scores = topk_scores / (jnp.sum(topk_scores, axis=-1, keepdims=True) + 1e-08)
        onehot = jax.nn.one_hot(topk_idx, NUM_EXPERTS, dtype=x.dtype)
        combine_w = jnp.einsum('bsk,bske->bse', topk_scores, onehot)
        output = jnp.zeros_like(x)
        for e in range(NUM_EXPERTS):
            h = jax.nn.gelu(x @ W1[e] + b1[e])
            y = h @ W2[e] + b2[e]
            output = output + y * combine_w[..., e:e + 1]
        return output
    x = L0_attn_x
    x = x + 0.5 * _L0_ffn_ref(_layernorm(x, axis=-1), L0_ffn_router_w, L0_ffn_w1, L0_ffn_w3, L0_ffn_w2)
    x = x + _L0_attn_ref(_layernorm(x, axis=-1), L0_attn_Wq, L0_attn_bq, L0_attn_Wk, L0_attn_bk, L0_attn_Wv, L0_attn_bv, L0_attn_Wo, L0_attn_bo)
    x = x + 0.5 * _L0_ffn_ref(_layernorm(x, axis=-1), L0_ffn_router_w, L0_ffn_w1, L0_ffn_w3, L0_ffn_w2)
    x = x + 0.5 * _L1_ffn_ref(_layernorm(x, axis=-1), L1_ffn_Wg, L1_ffn_bg, L1_ffn_W1, L1_ffn_b1, L1_ffn_W2, L1_ffn_b2)
    x = x + _L1_attn_ref(_layernorm(x, axis=-1), L1_attn_ln_w, L1_attn_ln_b, L1_attn_W_qkv, L1_attn_b_qkv, L1_attn_W_proj, L1_attn_b_proj)
    x = x + 0.5 * _L1_ffn_ref(_layernorm(x, axis=-1), L1_ffn_Wg, L1_ffn_bg, L1_ffn_W1, L1_ffn_b1, L1_ffn_W2, L1_ffn_b2)
    return x

_drawn_inputs = setup_inputs


def setup_inputs(seed=0):
    import zlib

    import numpy as np

    out = dict(_drawn_inputs(seed))
    spreads = {'L1_attn_ln_w': (1.0, 0.6),
     'L1_attn_ln_b': (0.0, 0.8),
     'L1_attn_b_qkv': (0.0, 0.663),
     'L1_attn_b_proj': (0.0, 0.292)}
    factors = {'L0_attn_bq': 8.0,
     'L0_attn_bk': 64.0,
     'L1_attn_W_qkv': 8.0,
     'L1_attn_W_proj': 4.731,
     'L1_ffn_bg': 2.766,
     'L1_ffn_b1': 5.943,
     'L1_ffn_b2': 4.285}
    for name, (base, spread) in spreads.items():
        noise = np.random.default_rng([zlib.crc32(name.encode()), seed]).standard_normal(out[name].shape)
        drawn = base * np.exp(spread * noise) if base else spread * noise
        out[name] = jnp.asarray(drawn.astype(out[name].dtype))
    for name, factor in factors.items():
        out[name] = (out[name] * factor).astype(out[name].dtype)
    return out
```

```python
from contextlib import ExitStack

import concourse.bass as bass
from concourse import mybir

ALU = mybir.AluOpType
ACT = mybir.ActivationFunctionType
F32 = mybir.dt.float32
F16 = mybir.dt.float16
BF16 = mybir.dt.bfloat16
AX = mybir.AxisListType.X

P = 128
D = 128
T = 512
NS = T // P
NH = 16
DH = D // NH
NG = 4
HG = NH // NG
ST = P // HG
MROW = 3 * DH
E = 8
WIN = 32
QB = P - WIN
NB = -(-T // QB)
HB = NB // 2
PADL = WIN
TP = NB * QB
TK = PADL + TP
WS = 64.0
LN_EPS = 1e-5
NEG = -1e30
SCALE = DH ** -0.5
SLOTS = 2

STAGES = 6
MAINS = STAGES * SLOTS
KIND = ["ffn0", "win", "ffn0", "ffn1", "full", "ffn1"]
CH = {"ffn0": 2, "ffn1": 4}
LEAD = {"ffn0": 2, "ffn1": 3}


def kind(n):
    return KIND[n // SLOTS]


def is_ffn(n):
    return kind(n).startswith("ffn")


FF = [n for n in range(MAINS) if is_ffn(n)]
AT = [n for n in range(MAINS) if not is_ffn(n)]
CBASE = [sum(E * CH[kind(m)] for m in FF if m < n) for n in range(MAINS + 1)]
LNBASE = [sum(2 if kind(m) == "full" else 1 for m in range(n)) for n in range(MAINS + 1)]
C0 = E * CH["ffn0"]
UNITS = {"win": 4, "full": 2 * NS}
UBASE = [sum(NG * UNITS[kind(m)] for m in AT if m < n) for n in range(MAINS + 1)]
LITTLE = 22
DVE_STEPS = 152


def build(nc, x, Wq, bq, Wk, bk, Wv, bv, Wo, bo, rw0, w1, w3, w2, lnw, lnb, Wqkv, bqkv, Wproj, bproj,
          Wg, bg, W1, b1, W2, b2, out):
    SEQS = x.shape[0]
    BODIES = SEQS // SLOTS
    F0, F1 = w1.shape[2], W1.shape[2]
    assert x.shape[1:] == (T, D) and F0 == CH["ffn0"] * P and F1 == CH["ffn1"] * P and SEQS % SLOTS == 0

    ctx = ExitStack()
    with ctx:
        def sb(name, shape, dt=F32):
            return ctx.enter_context(nc.sbuf_tensor(name, shape, dt))

        def sem(name):
            return ctx.enter_context(nc.semaphore(name))

        w1s = sb("w1s", [P, 2, E * F0], F16)
        w3s = sb("w3s", [P, 2, E * F0], F16)
        w2s = sb("w2s", [P, 2, E * F0], F16)
        W1s = sb("W1s", [P, 2, E * F1], F16)
        W2s = sb("W2s", [P, 2, E * F1], F16)
        wqk = sb("wqk", [P, 2, 2, 2 * NG * P], F16)
        wv = sb("wv", [P, 2, 2, D], F16)
        wo = sb("wo", [P, 2, 2, D], F16)
        wr = sb("wr", [P, 2, 2, E], F16)
        b2s = sb("b2s", [2 * E, 2, D], F16)
        sel = sb("sel", [2 * E, E, P], F16)
        qkb = sb("qkb", [P, 2, 2 * NG])
        lom = sb("lom", [P, 2])
        b1c = sb("b1c", [P, E * CH["ffn1"]])
        bvb = sb("bvb", [P, 2, D])
        bob = sb("bob", [P, 2, D])
        bgb = sb("bgb", [P, E])
        lnwb = sb("lnwb", [P, D])
        lnbb = sb("lnbb", [P, D])
        tri = sb("tri", [P, E, E])
        ident = sb("ident", [P, P])
        ident16 = sb("ident16", [P, P], F16)
        identb = sb("identb", [P, P], BF16)
        maskq = sb("maskq", [P, 2, HB, P], BF16)
        maskk = sb("maskk", [P, 2, HB, QB], BF16)
        mhalf = sb("mhalf", [P, NS])

        xin = sb("xin", [P, SLOTS, NS, D])
        xw = sb("xw", [P, SLOTS, NS, D])
        xn = sb("xn", [P, SLOTS, NS, D])
        zz = sb("zz", [P, SLOTS, NS, D])
        xT = sb("xT", [P, SLOTS, 2, TK], F16)
        cT = sb("cT", [2 * E, SLOTS, T], F16)
        st6 = sb("st6", [P, NS, 6])
        mv = sb("mv", [P, NS, 2])
        ve = sb("ve", [P, NS])
        rstd = sb("rstd", [P, NS])
        lg = sb("lg", [P, NS, E])
        mx = sb("mx", [P, NS])
        ex = sb("ex", [P, NS, E])
        gt = sb("gt", [P, NS, E, E])
        eq = sb("eq", [P, NS, E, E])
        rank = sb("rank", [P, NS, E])
        cw = sb("cw", [P, NS, E])
        zs = sb("zs", [P, NS])
        ssum = sb("ssum", [P, NS])
        c2 = sb("c2", [P, NS, 2 * E], F16)
        act = sb("act", [P, 2, T])
        hi = sb("hi", [P, 4, T], F16)
        lo = sb("lo", [P, 4, T], F16)
        cbs = sb("cbs", [P, 2, T])
        yc = sb("yc", [P, 2, T])
        zero = sb("zero", [P, T])
        acc = sb("acc", [P, 2, T])
        q3 = sb("q3", [P, NG, TP], F16)
        q3m = sb("q3m", [P, 2, TP], F16)
        k3 = sb("k3", [P, NG, TK], F16)
        qk32 = sb("qk32", [P, 2, T])
        qk16 = sb("qk16", [P, 2, T], F16)
        v4 = sb("v4", [P, NB, NH, ST])
        mxs = sb("mxs", [P, 2, HG, NB])
        mp = sb("mp", [P, 2, NB, P], F16)
        pT = sb("pT", [P, 2, 2, T])
        oT = sb("oT", [P, 2, TP])
        rec = sb("rec", [P, NS, HG])
        ao = sb("ao", [P, NS, NH, DH])
        aT = sb("aT", [P, 2, T], F16)
        stage = sb("stage", [P, 2, E * F0])
        small = zz
        smallT = xn[:, 0]
        rows = acc[0:1].rearrange("p a (b d) -> p (a b) d", d=D)
        qkrow = xn[0:1, 1]
        brow = pT[0:1]
        rstage = sb("rstage", [P, 2, E])
        b1st = sb("b1st", [E * CH["ffn1"], P])
        b2st = sb("b2st", [2 * E, D])
        lrow = sb("lrow", [1, 2, P])
        ones = sb("ones", [1, P])

        U = ctx.enter_context(nc.psum_tensor("U", [P, 4, T], F32))
        Y = ctx.enter_context(nc.psum_tensor("Y", [P, 2, T], F32))
        T0 = ctx.enter_context(nc.psum_tensor("T0", [P, T], F32))
        T1 = ctx.enter_context(nc.psum_tensor("T1", [P, T], F32))
        T0h = T0[:].bitcast(F16)
        T1h = T1[:].bitcast(F16)

        per_body, loop_sems = {}, []

        def signal(name, times):
            s = sem(name)
            per_body[s.name] = times
            loop_sems.append(s)
            return s

        NFF, NAT = len(FF), len(AT)
        s_xin = [sem("xin_loaded0"), sem("xin_loaded1")]
        s_out = sem("out_stored")
        s_var = signal("variance_ready", LNBASE[MAINS])
        s_rstd = signal("rstd_ready", LNBASE[MAINS])
        s_xn = signal("norm_ready", MAINS)
        s_xt = signal("normT_in_psum", MAINS)
        s_xh = signal("normT_hi_ready", MAINS)
        s_xl = signal("normT_lo_ready", MAINS)
        s_lg = signal("logits_in_psum", NFF)
        s_ls = signal("logits_shifted", NFF)
        s_ex = signal("router_exp_ready", NFF)
        s_c2 = signal("combine_ready", NFF)
        s_cp = signal("combineT_in_psum", NFF)
        s_ct = signal("combineT_ready", NFF)
        s_up = signal("up_in_psum", CBASE[MAINS])
        s_gt = signal("gate_in_psum", NFF // 2 * C0)
        s_si = signal("silu_ready", NFF // 2 * C0)
        s_pr = signal("gated_ready", NFF // 2 * C0)
        s_hi = signal("gated_hi_ready", NFF // 2 * C0)
        s_hf = signal("hidden_ready", NFF // 2 * E * CH["ffn1"])
        s_lo = signal("hidden_lo_ready", CBASE[MAINS])
        s_dn = signal("down_done", CBASE[MAINS])
        s_cb = signal("combine_bcast_in_psum", NFF * E)
        s_cs = signal("combine_bcast_ready", NFF * E)
        s_yc = signal("weighted_ready", NFF * E)
        s_ac = signal("accumulated", NFF * E)
        s_b2 = signal("bias2_in_psum", NFF // 2)
        s_b2c = signal("bias2_ready", NFF // 2)
        s_fin = signal("result_in_psum", MAINS)
        s_x = signal("residual_done", MAINS)
        s_pj = signal("proj_in_psum", NAT * 2 * NG)
        s_pb = signal("proj_biased", NAT * 2 * NG)
        s_qk = signal("strips_ready", NAT * 2 * NG)
        s_vp = signal("v_in_psum", NAT)
        s_v = signal("v_ready", NAT)
        s_sa = signal("scores_for_max", UBASE[MAINS])
        s_mx = signal("max_taken", UBASE[MAINS])
        s_mp = signal("neg_max_ready", NAT * NG)
        s_mt = signal("neg_maxT_in_psum", NAT * NG)
        s_qm = signal("q_with_max_ready", NAT * NG)
        s_sc = signal("scores_in_psum", UBASE[MAINS])
        s_pe = signal("probs_ready", UBASE[MAINS])
        s_pv = signal("probs_used", UBASE[MAINS])
        s_o = signal("attn_outT_ready", NAT * NG)
        s_ot = signal("attn_out_in_psum", NAT * NG)
        s_ao = signal("attn_out_normed", NAT * NG)
        s_at = signal("attnT_in_psum", NAT)
        s_ah = signal("attnT_hi_ready", NAT)
        s_al = signal("attnT_lo_ready", NAT)
        s_dve = signal("vector_step", DVE_STEPS)
        s_ld = sem("weights_loaded")
        s_big = [sem("stage_loaded0"), sem("stage_loaded1")]
        s_su = sem("setup_vector_step")
        s_sg = sem("setup_gpsimd_step")
        s_sp = sem("setup_product_in_psum")
        s_go = sem("setup_done")
        s_rows = sem("setup_rows_identities_ready")
        s_hs = sem("setup_hi_ready")
        s_los = sem("setup_lo_ready")

        def count(it, s, n):
            return it * per_body[s.name] + max(n, 0) + 1

        def chunk(n, q):
            return CBASE[n] + q

        def fi(n):
            return FF.index(n)

        def ai(n):
            return AT.index(n)

        def gated(n, q):
            return fi(n) * C0 + q

        def plain(n, q):
            return (fi(n) - NFF // 2) * E * CH["ffn1"] + q

        def unit(n, g, u):
            return UBASE[n] + g * UNITS[kind(n)] + u

        def xres(n):
            return xin[:, n % SLOTS] if n < SLOTS else xw[:, n % SLOTS]

        def flat(ap):
            return ap.rearrange("p a b -> p (a b)")

        def strip(j):
            return slice(ST * j, ST * (j + 1))

        def walk(n, body):
            return {("v",): 0, ("first",): 1, (0, "mid"): 2, (0, "end"): 3, (1, "mid"): 4, (1, "end"): 5,
                    (2, "end"): 6, (3, "end"): 7}.get(body)

        block = ctx.enter_context(nc.Block())

        big = [(w1.rearrange("e h f -> h e f"), w1s, 0), (w3.rearrange("e h f -> h e f"), w3s, 0),
               (w2.rearrange("e (c f) d -> f (e c) d", f=P), w2s, 0)]
        for k in range(F1 // F0):
            es = slice(k * E * F0 // F1, (k + 1) * E * F0 // F1)
            big.append((W1[es].rearrange("e h f -> h e f"), W1s, k * E * F0))
            big.append((W2[es].rearrange("e (c f) d -> f (e c) d", f=P), W2s, k * E * F0))

        def row(v):
            return v.rearrange("(a n) -> a n", a=1)

        SETUP_DONE = 3

        @block.sync
        def _(sp):
            xv = x.rearrange("b (s p) d -> b p s d", p=P)
            ov = out.rearrange("b (s p) d -> b p s d", p=P)
            little = [(small[:, 0, 0], Wq), (small[:, 0, 1], Wk), (small[:, 0, 2], Wv), (small[:, 0, 3], Wo),
                      (small[:, 1, 0:3], Wqkv.rearrange("p (a b) -> p a b", b=D)), (small[:, 1, 3], Wproj),
                      (rstage[:, 0], rw0), (rstage[:, 1], Wg),
                      (b1st[:], b1.rearrange("e (c f) -> (e c) f", f=P)), (b2st[0:E], b2), (b2st[E:2 * E], b2),
                      (rows[:, 0], row(bv)), (rows[:, 1], row(bqkv[2 * D:3 * D])), (rows[:, 2], row(bo)),
                      (rows[:, 3], row(bproj)), (rows[:, 4], row(lnw)), (rows[:, 5], row(lnb)),
                      (rows[:, 6, 0:E], row(bg)), (qkrow[:, 0], row(bq)), (qkrow[:, 1], row(bk)),
                      (qkrow[:, 2], row(bqkv[0:D])), (qkrow[:, 3], row(bqkv[D:2 * D]))]
            assert len(little) == LITTLE
            for dst, src in little:
                sp.dma_start(dst, src).then_inc(s_ld, 16)
            for a in range(SLOTS):
                sp.dma_start(xin[:, a], xv[a]).then_inc(s_xin[a], 16)
            for k, (src, _, _) in enumerate(big):
                if k >= 2:
                    sp.wait_ge(s_los, k - 1)
                sp.dma_start(stage[:, k % 2].rearrange("p (a b) -> p a b", a=src.shape[1]), src)\
                  .then_inc(s_big[k % 2], 16)

            def load(it):
                for a in range(SLOTS):
                    sp.wait_ge(s_x, count(it, s_x, a + 1))
                    sp.dma_start(xin[:, a], xv[bass.ds((it + 1) * SLOTS + a, 1)].rearrange(
                        "o p s d -> p (o s) d")).then_inc(s_xin[a], 16)

            def store(it):
                for a in range(SLOTS):
                    sp.wait_ge(s_x, count(it, s_x, MAINS - SLOTS + a + 1))
                    sp.dma_start(ov[bass.ds(it * SLOTS + a, 1)].rearrange("o p s d -> p (o s) d"),
                                 xw[:, a]).then_inc(s_out, 16)

            with sp.Fori(0, BODIES - 1) as it:
                load(it)
                store(it)
            store(BODIES - 1)
            sp.wait_ge(s_out, 16 * SEQS + 1)

        @block.tensor
        def _(pe):
            mm = nc.tensor.matmul

            def product(o, weights, moving, first=True, last=True, **kw):
                terms = [(0, 0), (1, 0), (0, 1)]
                for k, (i, j) in enumerate(terms):
                    ins = mm(o, weights(i), moving(j), start=first and k == 0, stop=last and k == 2, **kw)
                return ins

            def tokens(a, j):
                return xT[:, a, j, PADL:PADL + T]

            def turn(ps, src, width, ident_, at):
                return nc.tensor.transpose(ps[:, at:at + width], src, ident_)

            pe.wait_ge(s_ld, 16 * LITTLE)
            pe.wait_ge(s_rows, 2)
            for w in range(4):
                ins = turn(U[:, 0], small[:, 0, w], P, ident[:], w * P)
            ins.then_inc(s_sp, 1)
            mm(U[:, 1], ones[:], flat(rows[:, 0:4]), start=True, stop=True)
            mm(U[:, 2, 0:2 * D + E], ones[:], flat(rows[:, 4:7])[:, 0:2 * D + E], start=True, stop=True).then_inc(s_sp, 1)
            for l in range(2):
                for k in range(2 * NG):
                    mm(U[:, 3, l * 2 * NG + k:l * 2 * NG + k + 1],
                       brow[:, l, k // NG, (k % NG) * P:(k % NG + 1) * P], ones[:, 0:1], start=True, stop=True)
            for k in range(2):
                ins = mm(U[:, 3, 4 * NG + k:4 * NG + k + 1], lrow[:, k], ones[:, 0:1], start=True, stop=True)
            ins.then_inc(s_sp, 1)
            nc.tensor.transpose(Y[:, 0, 0:E * CH["ffn1"]], b1st[:], ident[0:E * CH["ffn1"], 0:E * CH["ffn1"]])\
              .then_inc(s_sp, 1)
            pe.wait_ge(s_go, SETUP_DONE)

            def hook(it, n, pos):
                m = n + 1
                if pos == 0 and n >= 1 and is_ffn(n - 1):
                    pe.wait_ge(s_ac, count(it, s_ac, (fi(n - 1) + 1) * E))
                    for s in range(NS):
                        ins = turn(T1, acc[:, (n - 1) % 2, s * P:(s + 1) * P], P, ident[:], s * P)
                    ins.then_inc(s_fin, 1)
                if m >= MAINS:
                    return
                if pos == 3:
                    pe.wait_ge(s_xn, count(it, s_xn, m + 1))
                    for s in range(NS):
                        ins = turn(T1, xn[:, m % 2, s], P, ident[:], s * P)
                    ins.then_inc(s_xt, 1)
                if pos == 5 and is_ffn(m):
                    pe.wait_ge(s_xl, count(it, s_xl, m + 1))
                    r = 0 if kind(m) == "ffn0" else 1
                    for s in range(NS):
                        at = PADL + s * P
                        ins = product(T1[:, s * E:(s + 1) * E], lambda i: xT[:, m % 2, i, at:at + P],
                                      lambda j: wr[:, r, j])
                    ins.then_inc(s_lg, 1)
                if pos == 7 and is_ffn(m):
                    pe.wait_ge(s_c2, count(it, s_c2, fi(m) + 1))
                    for s in range(NS):
                        ins = nc.tensor.transpose(T1h[0:2 * E, s * P:(s + 1) * P], c2[:, s], ident16[:])
                    ins.then_inc(s_cp, 1)

            def prior_read(it, n):
                if n and is_ffn(n - 1):
                    pe.wait_ge(s_yc, count(it, s_yc, (fi(n - 1) + 1) * E))
                    pe.wait_ge(s_cs, count(it, s_cs, (fi(n - 1) + 1) * E))
                elif n:
                    pe.wait_ge(s_x, count(it, s_x, n))

            def ffn(it, n):
                a, k = n % 2, kind(n)
                C, L, nch = CH[k], LEAD[k], E * CH[k]
                W = W1s if k == "ffn1" else w1s
                V = W2s if k == "ffn1" else w2s

                def cols(w, q):
                    return lambda i: w[:, i, q * P:(q + 1) * P]

                def gate(q):
                    if q >= 2:
                        pe.wait_ge(s_si, count(it, s_si, gated(n, q - 2) + 1))
                    product(U[:, 2 * (q % 2)], cols(w1s, q), lambda j: tokens(a, j)).then_inc(s_gt, 1)

                def up(q):
                    if k == "ffn0":
                        if q >= 2:
                            pe.wait_ge(s_lo, count(it, s_lo, chunk(n, q - 2) + 1))
                        product(U[:, 2 * (q % 2) + 1], cols(w3s, q), lambda j: tokens(a, j)).then_inc(s_up, 1)
                    else:
                        if q >= 4:
                            pe.wait_ge(s_lo, count(it, s_lo, chunk(n, q - 4) + 1))
                        product(U[:, q % 4], cols(W, q), lambda j: tokens(a, j)).then_inc(s_up, 1)

                def broadcast(e):
                    if e:
                        pe.wait_ge(s_cs, count(it, s_cs, fi(n) * E + e))
                    elif k == "ffn1":
                        mm(T0[:], b2s[:, 0], cT[:, a], start=True, stop=False)
                        mm(T0[:], b2s[:, 1], cT[:, a], start=False, stop=True).then_inc(s_b2, 1)
                        pe.wait_ge(s_b2c, count(it, s_b2c, fi(n) - NFF // 2 + 1))
                    mm(T0[:], sel[:, e], cT[:, a], start=True, stop=True).then_inc(s_cb, 1)

                pe.wait_ge(s_ct, count(it, s_ct, fi(n) + 1))
                for q in range(L):
                    if k == "ffn0":
                        gate(q)
                    up(q)
                prior_read(it, n)
                for q in range(nch):
                    e = q // C
                    if k == "ffn0" and q + L < nch:
                        gate(q + L)
                    if q + L < nch:
                        up(q + L)
                    if q % C == 0:
                        broadcast(e)
                        if e >= 2:
                            pe.wait_ge(s_yc, count(it, s_yc, fi(n) * E + e - 1))
                    pe.wait_ge(s_lo, count(it, s_lo, chunk(n, q) + 1))
                    Q = chunk(n, q)
                    product(Y[:, e % 2], cols(V, q), lambda j: (lo if j else hi)[:, Q % 4],
                            first=q % C == 0, last=q % C == C - 1).then_inc(s_dn, 1)
                    if q % C == C - 1:
                        hook(it, n, e)

            def attention(it, n):
                a, k, i = n % 2, kind(n), ai(n)
                l = 0 if k == "win" else 1
                full = k == "full"
                nu = UNITS[k]
                pe.wait_ge(s_xl, count(it, s_xl, n + 1))
                prior_read(it, n)
                for p in range(2 * NG):
                    if p >= 4:
                        pe.wait_ge(s_pb, count(it, s_pb, i * 2 * NG + p - 3))
                    product(U[:, p % 4], lambda i_: wqk[:, l, i_, p * P:(p + 1) * P],
                            lambda j: tokens(a, j)).then_inc(s_pj, 1)
                for b in range(NS if full else NB):
                    at = PADL + b * P if full else b * QB
                    o = Y[:, 0, b * P:(b + 1) * P] if full else Y[:, b // HB, (b % HB) * P:(b % HB + 1) * P]
                    ins = product(o, lambda i_: xT[:, a, i_, at:at + P], lambda j: wv[:, l, j])
                ins.then_inc(s_vp, 1)
                hook(it, n, walk(n, ("v",)))
                pe.wait_ge(s_pb, count(it, s_pb, (i + 1) * 2 * NG))

                def for_max(g, u):
                    pe.wait_ge(s_qk, count(it, s_qk, i * 2 * NG + NG + g + 1))
                    pe.wait_ge(s_mx, count(it, s_mx, unit(n, g, u)))
                    for jj in range(2):
                        j = 2 * (u % 2) + jj
                        r = strip(j)
                        if full:
                            qs = u // 2
                            ins = mm(U[:, jj], q3[r, g, qs * P:(qs + 1) * P], k3[r, g, PADL:PADL + T],
                                     start=True, stop=True)
                        else:
                            half = u // 2
                            mm(U[0:QB, jj, 0:HB * P], identb[:, 0:QB], flat(maskq[:, half]), start=True, stop=False)
                            for b in range(HB):
                                at = (half * HB + b) * QB
                                ins = mm(U[0:QB, jj, b * P:(b + 1) * P], q3[r, g, at:at + QB], k3[r, g, at:at + P],
                                         start=False, stop=b == HB - 1)
                    ins.then_inc(s_sa, 1)

                def scores(g, u):
                    pe.wait_ge(s_qm, count(it, s_qm, i * NG + g + 1))
                    pe.wait_ge(s_pe, count(it, s_pe, unit(n, g, u)))
                    for jj in range(2):
                        j = 2 * (u % 2) + jj
                        r = strip(j)
                        if full:
                            ks = PADL + u // 2 * P
                            ins = mm(U[:, 2 + jj], k3[r, g, ks:ks + P], q3m[r, g % 2, 0:T], start=True, stop=True)
                        else:
                            half = u // 2
                            mm(U[:, 2 + jj, 0:HB * QB], identb[:], flat(maskk[:, half]), start=True, stop=False)
                            for b in range(HB):
                                at = (half * HB + b) * QB
                                ins = mm(U[:, 2 + jj, b * QB:(b + 1) * QB], k3[r, g, at:at + P],
                                         q3m[r, g % 2, at:at + QB], start=False, stop=b == HB - 1)
                    ins.then_inc(s_sc, 1)

                def values(g, u):
                    pe.wait_ge(s_v, count(it, s_v, i + 1))
                    pe.wait_ge(s_pe, count(it, s_pe, unit(n, g, u) + 1))
                    pe.wait_ge(s_o, count(it, s_o, i * NG + (g - 1 if full else g)))
                    for jj in range(2):
                        j = 2 * (u % 2) + jj
                        h = g * HG + j
                        if full:
                            ks = u // 2
                            ins = mm(Y[strip(j), g % 2], v4[:, ks, h], pT[:, u % 2, jj], start=ks == 0,
                                     stop=ks == NS - 1, tile_position=(0, ST * j))
                        else:
                            half = u // 2
                            for b in range(HB):
                                ins = mm(Y[strip(j), half, b * QB:(b + 1) * QB], v4[:, half * HB + b, h],
                                         pT[:, u % 2, jj, b * QB:(b + 1) * QB], start=True, stop=True,
                                         tile_position=(0, ST * j))
                    ins.then_inc(s_pv, 1)

                def turn_max(g):
                    pe.wait_ge(s_mp, count(it, s_mp, i * NG + g + 1))
                    pe.wait_ge(s_ao, count(it, s_ao, i * NG + g - 1))
                    for b in range(NS if full else NB):
                        w = P if full else QB
                        ins = nc.tensor.transpose(T0h[:, b * w:(b + 1) * w], mp[0:w, g % 2, b], ident16[0:w, 0:w])
                    ins.then_inc(s_mt, 1)

                def turn_out(g):
                    pe.wait_ge(s_o, count(it, s_o, i * NG + g + 1))
                    pe.wait_ge(s_qm, count(it, s_qm, i * NG + min(g + 2, NG)))
                    pe.wait_ge(s_ao, count(it, s_ao, i * NG + g))
                    for s in range(NS):
                        ins = turn(T0, oT[:, g % 2, s * P:(s + 1) * P], P, ident[:], s * P)
                    ins.then_inc(s_ot, 1)

                for u in range(nu):
                    for_max(0, u)
                turn_max(0)
                hook(it, n, walk(n, ("first",)))
                for g in range(NG):
                    for u in range(nu):
                        if g + 1 < NG:
                            for_max(g + 1, u)
                        scores(g, u)
                        if u:
                            values(g, u - 1)
                        if u == 2 and g:
                            turn_out(g - 1)
                        if u == nu // 2 - 1:
                            hook(it, n, walk(n, (g, "mid")))
                    values(g, nu - 1)
                    if g + 1 < NG:
                        turn_max(g + 1)
                    hook(it, n, walk(n, (g, "end")))
                turn_out(NG - 1)
                pe.wait_ge(s_ao, count(it, s_ao, (i + 1) * NG))
                for s in range(NS):
                    ins = turn(T0, flat(ao[:, s]), P, ident[:], s * P)
                ins.then_inc(s_at, 1)
                pe.wait_ge(s_al, count(it, s_al, i + 1))
                for s in range(NS):
                    ins = product(Y[:, 0, s * P:(s + 1) * P], lambda i_: aT[:, i_, s * P:(s + 1) * P],
                                  lambda j: wo[:, l, j])
                ins.then_inc(s_fin, 1)

            with pe.Fori(0, BODIES) as it:
                for pos in range(E):
                    hook(it, -1, pos)
                for n in range(MAINS):
                    (ffn if is_ffn(n) else attention)(it, n)
                hook(it, MAINS, 0)
                pe.wait_ge(s_x, count(it, s_x, MAINS))

        @block.scalar
        def _(eng):
            activate = nc.scalar.activation

            def copy(o, i, scale=1.0):
                return activate(o, i, ACT.Copy, scale=scale)

            for k, (_, dst, c) in enumerate(big):
                eng.wait_ge(s_big[k % 2], 16 * (k // 2 + 1))
                copy(dst[:, 0, c:c + E * F0], stage[:, k % 2], WS).then_inc(s_hs, 1)
            eng.sem_inc(s_go, 1)
            eng.wait_ge(s_go, SETUP_DONE)

            def hook(it, n, pos):
                m = n + 1
                if m >= MAINS:
                    return
                if pos == 4:
                    eng.wait_ge(s_xt, count(it, s_xt, m + 1))
                    copy(xT[:, m % 2, 0, PADL:PADL + T], T1[:]).then_inc(s_xh, 1)
                if pos == 6 and is_ffn(m):
                    eng.wait_ge(s_ls, count(it, s_ls, fi(m) + 1))
                    activate(flat(ex[:]), flat(cw[:]), ACT.Exp).then_inc(s_ex, 1)

            def ffn(it, n):
                k, i = kind(n), fi(n)
                C, L, nch = CH[k], LEAD[k], E * CH[k]

                def silu(q):
                    eng.wait_ge(s_gt, count(it, s_gt, gated(n, q) + 1))
                    eng.wait_ge(s_pr, count(it, s_pr, gated(n, q) - 1))
                    activate(act[:, q % 2], U[:, 2 * (q % 2)], ACT.Silu, scale=1 / WS).then_inc(s_si, 1)

                def spread(e):
                    if k == "ffn1" and e == 0:
                        eng.wait_ge(s_ac, count(it, s_ac, i * E))
                        eng.wait_ge(s_fin, count(it, s_fin, n - 1))
                        eng.wait_ge(s_b2, count(it, s_b2, i - NFF // 2 + 1))
                        copy(acc[:, n % 2], T0[:]).then_inc(s_b2c, 1)
                    eng.wait_ge(s_yc, count(it, s_yc, i * E + e - 1))
                    eng.wait_ge(s_cb, count(it, s_cb, i * E + e + 1))
                    copy(cbs[:, e % 2], T0[:]).then_inc(s_cs, 1)

                if k == "ffn0":
                    silu(0)
                    silu(1)
                for q in range(nch):
                    Q = chunk(n, q)
                    eng.wait_ge(s_dn, count(it, s_dn, Q - 3))
                    if k == "ffn0":
                        eng.wait_ge(s_pr, count(it, s_pr, gated(n, q) + 1))
                        copy(hi[:, Q % 4], U[:, 2 * (q % 2) + 1]).then_inc(s_hi, 1)
                        if q + 2 < nch:
                            silu(q + 2)
                        if q % C == 0:
                            spread(q // C)
                    else:
                        eng.wait_ge(s_up, count(it, s_up, Q + 1))
                        bias = b1c[:, q:q + 1]
                        activate(hi[:, Q % 4], U[:, q % 4], ACT.Gelu_apprx_tanh, bias=bias, scale=1 / WS)
                        activate(U[:, q % 4], U[:, q % 4], ACT.Gelu_apprx_tanh, bias=bias, scale=1 / WS)\
                            .then_inc(s_hf, 1)
                        if q >= L and (q - L) % C == 0:
                            spread((q - L) // C)
                    if q % C == 0 and q:
                        hook(it, n, q // C - 1)
                hook(it, n, E - 1)

            def attention(it, n):
                k, i = kind(n), ai(n)
                l = 0 if k == "win" else 1
                full = k == "full"
                nu = UNITS[k]
                w = T if full else HB * QB

                def out(g):
                    eng.wait_ge(s_pv, count(it, s_pv, unit(n, g, nu)))
                    eng.wait_ge(s_ot, count(it, s_ot, i * NG + g - 1))
                    if full:
                        copy(oT[:, g % 2, 0:T], Y[:, g % 2]).then_inc(s_o, 1)
                    else:
                        copy(oT[:, g % 2].rearrange("p (a b) -> p a b", a=2), Y[:, :, 0:w]).then_inc(s_o, 1)

                for p in range(2 * NG):
                    eng.wait_ge(s_pj, count(it, s_pj, i * 2 * NG + p + 1))
                    eng.wait_ge(s_qk, count(it, s_qk, i * 2 * NG + p - 1))
                    bias = qkb[:, l, p:p + 1]
                    activate(qk32[:, p % 2], U[:, p % 4], ACT.Identity, bias=bias, scale=1 / WS)
                    activate(qk16[:, p % 2], U[:, p % 4], ACT.Identity, bias=bias, scale=1 / WS)\
                        .then_inc(s_pb, 1)
                hook(it, n, walk(n, ("v",)))
                hook(it, n, walk(n, ("first",)))
                for g in range(NG):
                    for u in range(nu):
                        eng.wait_ge(s_sc, count(it, s_sc, unit(n, g, u) + 1))
                        eng.wait_ge(s_pv, count(it, s_pv, unit(n, g, u) - 1))
                        activate(pT[:, u % 2, :, 0:w], U[:, 2:4, 0:w], ACT.Exp, scale=SCALE).then_inc(s_pe, 1)
                        if u == 0 and g:
                            out(g - 1)
                        if u == nu // 2 - 1:
                            hook(it, n, walk(n, (g, "mid")))
                    hook(it, n, walk(n, (g, "end")))
                out(NG - 1)
                eng.wait_ge(s_at, count(it, s_at, i + 1))
                copy(aT[:, 0], T0[:]).then_inc(s_ah, 1)

            with eng.Fori(0, BODIES) as it:
                for pos in range(E):
                    hook(it, -1, pos)
                for n in range(MAINS):
                    (ffn if is_ffn(n) else attention)(it, n)

        @block.gpsimd
        def _(pool):
            g = nc.gpsimd
            done = [0]

            def step(ins):
                done[0] += 1
                ins.then_inc(s_sg, 1)
                pool.wait_ge(s_sg, done[0])

            for t in (ident, ident16, identb):
                step(g.memset(t[:], 0.0))
                step(g.affine_select(out=t[:], in_=t[:], compare_op=ALU.not_equal, fill=1.0, base=0,
                                     pattern=[[-1, P]], channel_multiplier=1))
            pool.sem_inc(s_rows, 1)
            step(g.memset(sel[:], 0.0))
            for base in (0, -E):
                step(g.affine_select(out=sel[:], in_=sel[:], compare_op=ALU.not_equal, fill=1.0, base=base,
                                     pattern=[[-1, E], [0, P]], channel_multiplier=1))

            def keep(t, base, pattern, mult):
                step(g.affine_select(out=t, in_=t, compare_op=ALU.is_ge, fill=NEG, base=base, pattern=pattern,
                                     channel_multiplier=mult))

            step(g.memset(maskq[:], 0.0))
            step(g.memset(maskk[:], 0.0))
            for half in range(2):
                keep(maskq[:, half], -1, [[0, HB], [1, P]], -1)
                keep(maskq[:, half], WIN, [[0, HB], [-1, P]], 1)
                keep(maskk[:, half], -1, [[0, HB], [-1, QB]], 1)
                keep(maskk[:, half], WIN, [[0, HB], [1, QB]], -1)
            keep(maskq[:, 0, 0], -PADL, [[1, P]], 0)
            keep(maskk[:, 0, 0], -PADL, [[0, QB]], 1)
            step(g.memset(tri[:], 0.0))
            for e in range(1, E):
                step(g.memset(tri[:, e, 0:e], 1.0))
            step(g.memset(mhalf[:], -0.5))
            step(g.memset(zero[:], 0.0))
            step(g.memset(xT[:], 0.0))
            step(g.memset(q3[:], 0.0))
            step(g.memset(k3[:], 0.0))
            step(g.memset(v4[:], 0.0))
            step(g.memset(v4[:, :, :, DH:DH + 1], 1.0))
            step(g.memset(mp[:], 0.0))
            for s in loop_sems + [s_out]:
                pool.sem_inc(s, 1)
            pool.sem_inc(s_go, 1)
            pool.wait_ge(s_go, SETUP_DONE)

            def hook(it, n, pos):
                m = n + 1
                if m < MAINS and pos == 1:
                    for k in range(LNBASE[m], LNBASE[m + 1]):
                        pool.wait_ge(s_var, count(it, s_var, k + 1))
                        g.tensor_tensor(rstd[:], ve[:], mhalf[:], ALU.pow).then_inc(s_rstd, 1)

            def ffn(it, n):
                i = fi(n)
                for e in range(E):
                    if e == 0:
                        pool.wait_ge(s_fin, count(it, s_fin, n - 1))
                        if kind(n) == "ffn1":
                            pool.wait_ge(s_b2c, count(it, s_b2c, i - NFF // 2 + 1))
                    pool.wait_ge(s_yc, count(it, s_yc, i * E + e + 1))
                    if e == 0 and kind(n) == "ffn0":
                        g.tensor_tensor(acc[:, n % 2], zero[:], yc[:, e % 2], ALU.add).then_inc(s_ac, 1)
                    else:
                        pool.wait_ge(s_ac, count(it, s_ac, i * E + e))
                        g.tensor_tensor(acc[:, n % 2], acc[:, n % 2], yc[:, e % 2], ALU.add).then_inc(s_ac, 1)
                    hook(it, n, e)

            with pool.Fori(0, BODIES) as it:
                hook(it, -1, 1)
                for n in range(MAINS):
                    if is_ffn(n):
                        ffn(it, n)
                    else:
                        hook(it, n, 1)

        @block.vector
        def _(v):
            vec = nc.vector
            done = [0]

            def link(ins):
                done[0] += 1
                ins.then_inc(s_su, 1)
                v.wait_ge(s_su, done[0])

            def split(dst_hi, dst_lo, src, scale=WS):
                link(vec.tensor_scalar(dst_hi, src, scale, None, ALU.mult))
                link(vec.scalar_tensor_tensor(dst_lo, src, scale, dst_hi, ALU.mult, ALU.subtract))

            link(vec.memset(wqk[:], 0.0))
            link(vec.memset(brow, 0.0))
            link(vec.memset(lrow[:], 0.0))
            link(vec.memset(ones[:], 1.0))
            v.wait_ge(s_ld, 16 * LITTLE)
            for l in range(2):
                for k in range(2):
                    dst = brow[:, l, k].rearrange("p (h r) -> p h r", r=ST)
                    for r in range(3):
                        link(vec.tensor_copy(dst[:, :, r * DH:(r + 1) * DH],
                                             qkrow[:, 2 * l + k].rearrange("p (h d) -> p h d", d=DH)))
                link(vec.memset(brow[:, l, 1].rearrange("p (h r) -> p h r", r=ST)[:, :, MROW:MROW + 1], 1.0))
            for k, r in ((0, 2), (1, 1)):
                link(vec.memset(lrow[:, k].rearrange("p (h r) -> p h r", r=ST)[:, :, r * DH:(r + 1) * DH], -1.0))
            v.sem_inc(s_rows, 1)
            v.wait_ge(s_sp, 1)
            link(vec.tensor_copy(flat(smallT), U[:, 0]))
            for l in range(2):
                src = smallT if l == 0 else small[:, 1]
                for k in range(2):
                    w = src[:, k].rearrange("p (h d) -> p h d", d=DH)
                    at = slice(k * NG * P, (k + 1) * NG * P)
                    dst = [wqk[:, l, part, at].rearrange("p (h r) -> p h r", r=ST) for part in range(2)]
                    for r in range(3):
                        rs = slice(r * DH, (r + 1) * DH)
                        split(dst[0][:, :, rs], dst[1][:, :, rs], w)
                split(wv[:, l, 0], wv[:, l, 1], src[:, 2])
                split(wo[:, l, 0], wo[:, l, 1], src[:, 3])
                split(wr[:, l, 0], wr[:, l, 1], rstage[:, l])
            split(b2s[:, 0], b2s[:, 1], b2st[:])
            v.wait_ge(s_sp, 4)
            link(vec.tensor_copy(flat(bvb[:]), U[:, 1, 0:2 * D]))
            link(vec.tensor_copy(flat(bob[:]), U[:, 1, 2 * D:4 * D]))
            link(vec.tensor_copy(lnwb[:], U[:, 2, 0:D]))
            link(vec.tensor_copy(lnbb[:], U[:, 2, D:2 * D]))
            link(vec.tensor_copy(bgb[:], U[:, 2, 2 * D:2 * D + E]))
            link(vec.tensor_copy(flat(qkb[:]), U[:, 3, 0:4 * NG]))
            link(vec.tensor_copy(lom[:], U[:, 3, 4 * NG:4 * NG + 2]))
            link(vec.tensor_copy(b1c[:], Y[:, 0, 0:E * CH["ffn1"]]))
            for k, (_, dst, c) in enumerate(big):
                v.wait_ge(s_hs, k + 1)
                vec.scalar_tensor_tensor(dst[:, 1, c:c + E * F0], stage[:, k % 2], WS, dst[:, 0, c:c + E * F0],
                                         ALU.mult, ALU.subtract).then_inc(s_los, 1)
            v.wait_ge(s_los, len(big))
            v.sem_inc(s_go, 1)
            v.wait_ge(s_go, SETUP_DONE)
            steps = [0]

            def bcast(ap, n_, axis=2):
                shape = list(ap.shape)
                return ap.unsqueeze(axis).broadcast_to(shape[:axis] + [n_] + shape[axis:])

            def hook(it, n, pos):
                m = n + 1

                def step(ins):
                    steps[0] += 1
                    ins.then_inc(s_dve, 1)
                    v.wait_ge(s_dve, count(it, s_dve, steps[0]))

                def moments(src):
                    for s in range(NS):
                        ins = vec.bn_stats(st6[:, s], src[:, s])
                    step(ins)
                    vec.memset(ve[:], 0.0)
                    for s in range(NS):
                        ins = vec.bn_aggr(mv[:, s], st6[:, s])
                    step(ins)
                    vec.tensor_scalar(ve[:], mv[:, :, 1], LN_EPS, None, ALU.add).then_inc(s_var, 1)

                def normalise(dst, src):
                    for s in range(NS):
                        ins = vec.tensor_scalar(dst[:, s], src[:, s], mv[:, s, 0:1], rstd[:, s:s + 1],
                                                ALU.subtract, ALU.mult)
                    return ins

                if pos == 1 and n >= 1 and is_ffn(n - 1):
                    b = n - 1
                    v.wait_ge(s_fin, count(it, s_fin, b + 1))
                    if b < SLOTS:
                        v.wait_ge(s_out, it * 16 * SLOTS + 1)
                    vec.scalar_tensor_tensor(flat(xw[:, b % 2]), T1[:], 0.5 / WS, flat(xres(b)), ALU.mult,
                                             ALU.add).then_inc(s_x, 1)
                    v.wait_ge(s_x, count(it, s_x, b + 1))
                if m >= MAINS:
                    return
                a = m % 2
                if pos == 1:
                    if m < SLOTS:
                        v.wait_ge(s_xin[a], it * 16 + 16)
                    moments(xres(m))
                if pos == 2:
                    v.wait_ge(s_rstd, count(it, s_rstd, LNBASE[m] + 1))
                    if kind(m) != "full":
                        normalise(xn[:, a], xres(m)).then_inc(s_xn, 1)
                    else:
                        step(normalise(zz[:, a], xres(m)))
                        moments(zz[:, a])
                        v.wait_ge(s_rstd, count(it, s_rstd, LNBASE[m] + 2))
                        step(normalise(xn[:, a], zz[:, a]))
                        step(vec.tensor_tensor(xn[:, a], xn[:, a], bcast(lnwb[:], NS, 1), ALU.mult))
                        vec.tensor_tensor(xn[:, a], xn[:, a], bcast(lnbb[:], NS, 1), ALU.add).then_inc(s_xn, 1)
                if pos == 4:
                    v.wait_ge(s_xh, count(it, s_xh, m + 1))
                    vec.tensor_tensor(xT[:, a, 1, PADL:PADL + T], T1[:], xT[:, a, 0, PADL:PADL + T],
                                      ALU.subtract).then_inc(s_xl, 1)
                if pos == 6 and is_ffn(m):
                    v.wait_ge(s_lg, count(it, s_lg, fi(m) + 1))
                    logits = T1[:, 0:NS * E].rearrange("p (s e) -> p s e", e=E)
                    if kind(m) == "ffn0":
                        step(vec.tensor_scalar(lg[:], logits, 1 / WS, None, ALU.mult))
                    else:
                        step(vec.scalar_tensor_tensor(lg[:], logits, 1 / WS, bcast(bgb[:], NS, 1), ALU.mult,
                                                      ALU.add))
                    step(vec.tensor_reduce(mx[:], lg[:], AX, ALU.max))
                    vec.tensor_tensor(cw[:], lg[:], bcast(mx[:], E), ALU.subtract).then_inc(s_ls, 1)
                    other, own = bcast(lg[:], E, 2), bcast(lg[:], E, 3)
                    vec.tensor_tensor(gt[:], other, own, ALU.is_gt)
                    step(vec.tensor_tensor(eq[:], other, own, ALU.is_equal))
                    step(vec.tensor_tensor(eq[:], eq[:], bcast(tri[:], NS, 1), ALU.mult))
                    step(vec.tensor_tensor(gt[:], gt[:], eq[:], ALU.add))
                    step(vec.tensor_reduce(rank[:], gt[:], AX, ALU.add))
                    v.wait_ge(s_ex, count(it, s_ex, fi(m) + 1))
                    step(vec.scalar_tensor_tensor(flat(cw[:]), flat(rank[:]), 1.5, flat(ex[:]), ALU.is_lt, ALU.mult))
                    step(vec.tensor_reduce(ssum[:], cw[:], AX, ALU.add))
                    if kind(m) == "ffn1":
                        step(vec.tensor_reduce(zs[:], ex[:], AX, ALU.add))
                        step(vec.scalar_tensor_tensor(ssum[:], zs[:], 1e-8, ssum[:], ALU.mult, ALU.add))
                    step(vec.reciprocal(ssum[:], ssum[:]))
                    step(vec.tensor_tensor(cw[:], cw[:], bcast(ssum[:], E), ALU.mult))
                    step(vec.tensor_copy(c2[:, :, 0:E], cw[:]))
                    vec.tensor_tensor(c2[:, :, E:2 * E], cw[:], c2[:, :, 0:E], ALU.subtract).then_inc(s_c2, 1)
                if pos == E and is_ffn(m):
                    v.wait_ge(s_cp, count(it, s_cp, fi(m) + 1))
                    vec.tensor_copy(cT[:, a], T1h[0:2 * E, 0:T]).then_inc(s_ct, 1)

            def ffn(it, n):
                k, i = kind(n), fi(n)
                C, nch = CH[k], E * CH[k]

                def low(q):
                    Q = chunk(n, q)
                    bank = 2 * (q % 2) + 1 if k == "ffn0" else q % 4
                    if k == "ffn0":
                        v.wait_ge(s_hi, count(it, s_hi, gated(n, q) + 1))
                    else:
                        v.wait_ge(s_hf, count(it, s_hf, plain(n, q) + 1))
                    vec.tensor_tensor(lo[:, Q % 4], U[:, bank], hi[:, Q % 4], ALU.subtract).then_inc(s_lo, 1)

                def weigh(e):
                    v.wait_ge(s_dn, count(it, s_dn, chunk(n, (e + 1) * C)))
                    v.wait_ge(s_cs, count(it, s_cs, i * E + e + 1))
                    v.wait_ge(s_ac, count(it, s_ac, i * E + e - 1))
                    vec.tensor_tensor(yc[:, e % 2], Y[:, e % 2], cbs[:, e % 2], ALU.mult).then_inc(s_yc, 1)

                lag = 1 if k == "ffn0" else 0
                for q in range(nch + lag):
                    if k == "ffn0" and q < nch:
                        v.wait_ge(s_si, count(it, s_si, gated(n, q) + 1))
                        v.wait_ge(s_up, count(it, s_up, chunk(n, q) + 1))
                        bank = U[:, 2 * (q % 2) + 1]
                        vec.scalar_tensor_tensor(bank, bank, 1 / WS, act[:, q % 2], ALU.mult, ALU.mult)\
                            .then_inc(s_pr, 1)
                    if q < lag:
                        continue
                    c = q - lag
                    low(c)
                    if c % C == 0 and c:
                        weigh(c // C - 1)
                        hook(it, n, c // C - 1)
                weigh(E - 1)
                hook(it, n, E - 1)
                hook(it, n, E)

            def attention(it, n):
                k, i = kind(n), ai(n)
                l = 0 if k == "win" else 1
                full = k == "full"
                nu = UNITS[k]
                nb, w, width = (NS, P, T) if full else (NB, QB, TP)

                for p in range(2 * NG):
                    v.wait_ge(s_pb, count(it, s_pb, i * 2 * NG + p + 1))
                    dst = q3[:, p, 0:T] if p < NG else k3[:, p - NG, PADL:PADL + T]
                    vec.scalar_tensor_tensor(dst, qk16[:, p % 2], lom[:, p // NG:p // NG + 1], qk32[:, p % 2],
                                             ALU.mult, ALU.add).then_inc(s_qk, 1)
                v.wait_ge(s_vp, count(it, s_vp, i + 1))
                for b in range(nb):
                    src = Y[:, 0, b * P:(b + 1) * P] if full else Y[:, b // HB, (b % HB) * P:(b % HB + 1) * P]
                    ins = vec.scalar_tensor_tensor(v4[:, b, :, 0:DH], src.rearrange("p (h d) -> p h d", d=DH), 1 / WS,
                                                   bvb[:, l].rearrange("p (h d) -> p h d", d=DH), ALU.mult, ALU.add)
                ins.then_inc(s_v, 1)
                hook(it, n, walk(n, ("v",)))

                def maxima(g, u):
                    v.wait_ge(s_sa, count(it, s_sa, unit(n, g, u) + 1))
                    j, b = 2 * (u % 2), u // 2
                    if full:
                        vec.tensor_reduce(mxs[:, g % 2, j:j + 2, b], U[:, 0:2], AX, ALU.max).then_inc(s_mx, 1)
                    else:
                        vec.tensor_reduce(mxs[0:QB, g % 2, j:j + 2, b * HB:(b + 1) * HB],
                                          U[0:QB, 0:2, 0:HB * P].rearrange("p j (b k) -> p j b k", k=P), AX,
                                          ALU.max).then_inc(s_mx, 1)

                def negate(g):
                    v.wait_ge(s_mx, count(it, s_mx, unit(n, g, nu)))
                    dst = mp[0:w, g % 2, 0:nb].rearrange("p b (j r) -> p b j r", r=ST)[:, :, :, MROW]
                    vec.tensor_scalar(dst, mxs[0:w, g % 2, :, 0:nb].rearrange("p j b -> p b j"), -1.0, None,
                                      ALU.mult).then_inc(s_mp, 1)

                def with_max(g):
                    v.wait_ge(s_mt, count(it, s_mt, i * NG + g + 1))
                    vec.tensor_tensor(q3m[:, g % 2, 0:width], T0h[:, 0:width], q3[:, g, 0:width], ALU.add)\
                        .then_inc(s_qm, 1)

                def normed(g):
                    v.wait_ge(s_ot, count(it, s_ot, i * NG + g + 1))
                    o = T0[:].rearrange("p (s j r) -> p s j r", j=HG, r=ST)
                    steps[0] += 1
                    vec.reciprocal(rec[:], o[:, :, :, DH]).then_inc(s_dve, 1)
                    v.wait_ge(s_dve, count(it, s_dve, steps[0]))
                    vec.tensor_tensor(ao[:, :, g * HG:(g + 1) * HG], o[:, :, :, 0:DH], bcast(rec[:], DH, 3),
                                      ALU.mult).then_inc(s_ao, 1)

                for u in range(nu):
                    maxima(0, u)
                negate(0)
                with_max(0)
                hook(it, n, walk(n, ("first",)))
                for g in range(NG):
                    for u in range(nu):
                        if g + 1 < NG:
                            maxima(g + 1, u)
                        if u == nu // 2 - 1:
                            hook(it, n, walk(n, (g, "mid")))
                    if g:
                        normed(g - 1)
                    if g + 1 < NG:
                        negate(g + 1)
                        with_max(g + 1)
                    hook(it, n, walk(n, (g, "end")))
                normed(NG - 1)
                v.wait_ge(s_ah, count(it, s_ah, i + 1))
                vec.tensor_tensor(aT[:, 1], T0[:], aT[:, 0], ALU.subtract).then_inc(s_al, 1)
                if full:
                    steps[0] += 1
                    vec.tensor_tensor(flat(xw[:, n % 2]), flat(xw[:, n % 2]), flat(zz[:, n % 2]), ALU.add)\
                        .then_inc(s_dve, 1)
                    v.wait_ge(s_dve, count(it, s_dve, steps[0]))
                steps[0] += 1
                vec.tensor_tensor(xw[:, n % 2], xw[:, n % 2], bcast(bob[:, l], NS, 1), ALU.add).then_inc(s_dve, 1)
                v.wait_ge(s_dve, count(it, s_dve, steps[0]))
                v.wait_ge(s_fin, count(it, s_fin, n + 1))
                vec.scalar_tensor_tensor(flat(xw[:, n % 2]), Y[:, 0], 1 / WS, flat(xw[:, n % 2]), ALU.mult,
                                         ALU.add).then_inc(s_x, 1)
                hook(it, n, E)

            with v.Fori(0, BODIES) as it:
                for pos in range(E + 1):
                    hook(it, -1, pos)
                for n in range(MAINS):
                    (ffn if is_ffn(n) else attention)(it, n)
                hook(it, MAINS, 1)
            assert steps[0] == DVE_STEPS, steps[0]


_INS = ['L0_attn_x', 'L0_attn_Wq', 'L0_attn_bq', 'L0_attn_Wk', 'L0_attn_bk', 'L0_attn_Wv', 'L0_attn_bv',
        'L0_attn_Wo', 'L0_attn_bo', 'L0_ffn_router_w', 'L0_ffn_w1', 'L0_ffn_w3', 'L0_ffn_w2',
        'L1_attn_ln_w', 'L1_attn_ln_b', 'L1_attn_W_qkv', 'L1_attn_b_qkv', 'L1_attn_W_proj',
        'L1_attn_b_proj', 'L1_ffn_Wg', 'L1_ffn_bg', 'L1_ffn_W1', 'L1_ffn_b1', 'L1_ffn_W2', 'L1_ffn_b2']


def kernel(**inputs):
    import numpy as _np
    import concourse.bacc as _bacc
    from concourse import mybir as _mybir
    from concourse.bass_utils import run_bass_kernel_spmd as _run

    nc = _bacc.Bacc("TRN2", target_bir_lowering=False, num_devices=1)
    arrays, args = {}, []
    for name in _INS:
        a = _np.ascontiguousarray(inputs[name])
        arrays[f"in_{name}_dram"] = a
        args.append(nc.dram_tensor(f"in_{name}_dram", a.shape, _mybir.dt.from_np(a.dtype), kind="ExternalInput").ap())
    shape = arrays["in_L0_attn_x_dram"].shape
    args.append(nc.dram_tensor("out_0_dram", shape, _mybir.dt.float32, kind="ExternalOutput").ap())
    build(nc, *args)
    r = _run(nc, [arrays], core_ids=[0])
    return r.results[0]["out_0_dram"]
```

```python
from contextlib import ExitStack

import concourse.bass as bass
from concourse import mybir

ALU = mybir.AluOpType
ACT = mybir.ActivationFunctionType
F32 = mybir.dt.float32
F16 = mybir.dt.float16
BF16 = mybir.dt.bfloat16
AX = mybir.AxisListType.X

P = 128
D = 128
T = 512
NS = T // P
NH = 16
DH = D // NH
NG = 4
HG = NH // NG
ST = P // HG
MROW = 3 * DH
E = 8
WIN = 32
QB = P - WIN
NB = -(-T // QB)
HB = NB // 2
PADL = WIN
TP = NB * QB
TK = PADL + TP
WS = 64.0
LN_EPS = 1e-5
NEG = -1e30
SCALE = DH ** -0.5
SLOTS = 2

POS = 16
STAGES = 6
MAINS = STAGES * SLOTS
KIND = ["ffn0", "win", "ffn0", "ffn1", "full", "ffn1"]
CH = {"ffn0": 2, "ffn1": 4}
LEAD = {"ffn0": 3, "ffn1": 3}


def kind(n):
    return KIND[n // SLOTS]


def is_ffn(n):
    return kind(n).startswith("ffn")


FF = [n for n in range(MAINS) if is_ffn(n)]
AT = [n for n in range(MAINS) if not is_ffn(n)]
CBASE = [sum(E * CH[kind(m)] for m in FF if m < n) for n in range(MAINS + 1)]
LNBASE = [sum(2 if kind(m) == "full" else 1 for m in range(n)) for n in range(MAINS + 1)]
C0 = E * CH["ffn0"]
TILES = {"win": NB // HB, "full": NS}
UNITS = {k: HG * t for k, t in TILES.items()}
UBASE = [sum(NG * UNITS[kind(m)] for m in AT if m < n) for n in range(MAINS + 1)]
LITTLE = 22
DVE_STEPS = 168


def build(nc, x, Wq, bq, Wk, bk, Wv, bv, Wo, bo, rw0, w1, w3, w2, lnw, lnb, Wqkv, bqkv, Wproj, bproj,
          Wg, bg, W1, b1, W2, b2, out):
    SEQS = x.shape[0]
    BODIES = SEQS // SLOTS
    F0, F1 = w1.shape[2], W1.shape[2]
    assert x.shape[1:] == (T, D) and F0 == CH["ffn0"] * P and F1 == CH["ffn1"] * P and SEQS % SLOTS == 0

    nc.disable_value_cache = True
    ctx = ExitStack()
    with ctx:
        def sb(name, shape, dt=F32):
            return ctx.enter_context(nc.sbuf_tensor(name, shape, dt))

        def sem(name):
            return ctx.enter_context(nc.semaphore(name))

        w1s = sb("w1s", [P, 2, E * F0], F16)
        w3s = sb("w3s", [P, 2, E * F0], F16)
        w2s = sb("w2s", [P, 2, E * F0], F16)
        W1s = sb("W1s", [P, 2, E * F1], F16)
        W2s = sb("W2s", [P, 2, E * F1], F16)
        wqk = sb("wqk", [P, 2, 2, 2 * NG * P], F16)
        wv = sb("wv", [P, 2, 2, D], F16)
        wo = sb("wo", [P, 2, 2, D], F16)
        wr = sb("wr", [P, 2, 2, E], F16)
        b2s = sb("b2s", [2 * E, 2, D], F16)
        sel = sb("sel", [2 * E, E, P], F16)
        qkb = sb("qkb", [P, 2, 2 * NG])
        lom = sb("lom", [P, 2])
        b1c = sb("b1c", [P, E * CH["ffn1"]])
        bvb = sb("bvb", [P, 2, D])
        bob = sb("bob", [P, 2, D])
        bgb = sb("bgb", [P, E])
        lnwb = sb("lnwb", [P, D])
        lnbb = sb("lnbb", [P, D])
        tri = sb("tri", [P, E, E])
        ident = sb("ident", [P, P])
        ident16 = sb("ident16", [P, P], F16)
        identb = sb("identb", [P, P], BF16)
        maskq = sb("maskq", [P, 2, HB, P], BF16)
        maskk = sb("maskk", [P, 2, HB, QB], BF16)
        mhalf = sb("mhalf", [P, NS])

        xin = sb("xin", [P, SLOTS, NS, D])
        xw = sb("xw", [P, SLOTS, NS, D])
        xn = sb("xn", [P, SLOTS, NS, D])
        zz = sb("zz", [P, SLOTS, NS, D])
        xT = sb("xT", [P, SLOTS, 2, TK], F16)
        cT = sb("cT", [2 * E, SLOTS, T], F16)
        st6 = sb("st6", [P, NS, 6])
        mv = sb("mv", [P, NS, 2])
        ve = sb("ve", [P, NS])
        rstd = sb("rstd", [P, NS])
        lg = sb("lg", [P, NS, E])
        mx = sb("mx", [P, NS])
        ex = sb("ex", [P, NS, E])
        gt = sb("gt", [P, NS, E, E])
        eq = sb("eq", [P, NS, E, E])
        rank = sb("rank", [P, NS, E])
        cw = sb("cw", [P, NS, E])
        zs = sb("zs", [P, NS])
        ssum = sb("ssum", [P, NS])
        c2 = sb("c2", [P, NS, 2 * E], F16)
        hidden = sb("hidden", [P, 2, 4, T], F16)
        hi, lo = hidden[:, 0], hidden[:, 1]
        cbs = sb("cbs", [P, 2, T])
        yc = sb("yc", [P, 2, T])
        zero = sb("zero", [P, T])
        acc = sb("acc", [P, 2, T])
        q3 = sb("q3", [P, NG, TP], F16)
        q3m = sb("q3m", [P, 2, TP], F16)
        k3 = sb("k3", [P, 2, T], F16)
        kz = sb("kz", [P, NH, TK], F16)
        smask = sb("smask", [P, HG])
        qk32 = sb("qk32", [P, 2, T])
        qk16 = sb("qk16", [P, 2, T], F16)
        v4 = sb("v4", [P, NB, NH, ST])
        mxs = sb("mxs", [P, 2, HG, NB])
        mp = sb("mp", [P, 2, NB, P], F16)
        pT = sb("pT", [P, 8, T])
        gated, act = pT[:, 0:4], pT[:, 4:8]
        oT = sb("oT", [P, 2, TP])
        rec = sb("rec", [P, NS, HG])
        ao = sb("ao", [P, NS, NH, DH])
        aT = sb("aT", [P, 2, T], F16)
        small = zz
        smallT = xn[:, 0]
        rows = acc[0:1].rearrange("p a (b d) -> p (a b) d", d=D)
        qkrow = xn[0:1, 1]
        brow = hidden[0:1].rearrange("p a b c -> p (a b c)").bitcast(F32).rearrange(
            "p (l k n) -> p l k n", l=2, k=2)
        stage = pT[:].rearrange("p (a b) c -> p a (b c)", a=2)
        rstage = sb("rstage", [P, 2, E])
        b1st = sb("b1st", [E * CH["ffn1"], P])
        b2st = sb("b2st", [2 * E, D])
        lrow = sb("lrow", [1, 2, P])
        ones = sb("ones", [1, P])

        U = ctx.enter_context(nc.psum_tensor("U", [P, 4, T], F32))
        Y = ctx.enter_context(nc.psum_tensor("Y", [P, 2, T], F32))
        T0 = ctx.enter_context(nc.psum_tensor("T0", [P, T], F32))
        T1 = ctx.enter_context(nc.psum_tensor("T1", [P, T], F32))
        T0h = T0[:].bitcast(F16)
        T1h = T1[:].bitcast(F16)

        per_body, loop_sems = {}, []

        def signal(name, times):
            s = sem(name)
            per_body[s.name] = times
            loop_sems.append(s)
            return s

        NFF, NAT = len(FF), len(AT)
        s_xin = [sem("xin_loaded0"), sem("xin_loaded1")]
        s_out = sem("out_stored")
        s_var = signal("variance_ready", LNBASE[MAINS])
        s_rstd = signal("rstd_ready", LNBASE[MAINS])
        s_xn = signal("norm_ready", MAINS)
        s_xt = signal("normT_in_psum", MAINS)
        s_xh = signal("normT_hi_ready", MAINS)
        s_xl = signal("normT_lo_ready", MAINS)
        s_lg = signal("logits_in_psum", NFF)
        s_ls = signal("logits_shifted", NFF)
        s_ex = signal("router_exp_ready", NFF)
        s_c2 = signal("combine_ready", NFF)
        s_cp = signal("combineT_in_psum", NFF)
        s_ct = signal("combineT_ready", NFF)
        s_up = signal("up_in_psum", CBASE[MAINS])
        s_gt = signal("gate_in_psum", NFF // 2 * C0)
        s_si = signal("silu_ready", NFF // 2 * C0)
        s_pr = signal("gated_ready", NFF // 2 * C0)
        s_hi = signal("gated_hi_ready", NFF // 2 * C0)
        s_hf = signal("hidden_ready", NFF // 2 * E * CH["ffn1"])
        s_lo = signal("hidden_lo_ready", CBASE[MAINS])
        s_dn = signal("down_done", CBASE[MAINS])
        s_cb = signal("combine_bcast_in_psum", NFF * E)
        s_cs = signal("combine_bcast_ready", NFF * E)
        s_yc = signal("weighted_ready", NFF * E)
        s_ac = signal("accumulated", NFF * E)
        s_b2 = signal("bias2_in_psum", NFF // 2)
        s_b2c = signal("bias2_ready", NFF // 2)
        s_fin = signal("result_in_psum", MAINS)
        s_x = signal("residual_done", MAINS)
        s_pj = signal("proj_in_psum", NAT * 2 * NG)
        s_pb = signal("proj_biased", NAT * 2 * NG)
        s_qk = signal("strips_ready", NAT * 2 * NG)
        s_kt = signal("k_strips_unmasked", NAT * NG)
        s_vp = signal("v_in_psum", NAT)
        s_v = signal("v_ready", NAT)
        s_sa = signal("scores_for_max", UBASE[MAINS])
        s_mx = signal("max_taken", UBASE[MAINS])
        s_mp = signal("neg_max_ready", NAT * NG)
        s_mt = signal("neg_maxT_in_psum", NAT * NG)
        s_qm = signal("q_with_max_ready", NAT * NG)
        s_sc = signal("scores_in_psum", UBASE[MAINS])
        s_pe = signal("probs_ready", UBASE[MAINS])
        s_pv = signal("probs_used", UBASE[MAINS] // HG)
        s_o = signal("attn_outT_ready", NAT * NG)
        s_ot = signal("attn_out_in_psum", NAT * NG)
        s_ao = signal("attn_out_normed", NAT * NG)
        s_at = signal("attnT_in_psum", NAT)
        s_ah = signal("attnT_hi_ready", NAT)
        s_al = signal("attnT_lo_ready", NAT)
        s_dve = signal("vector_step", DVE_STEPS)
        s_ld = sem("weights_loaded")
        s_big = [sem("stage_loaded0"), sem("stage_loaded1")]
        s_su = sem("setup_vector_step")
        s_sg = sem("setup_gpsimd_step")
        s_sp = sem("setup_product_in_psum")
        s_go = sem("setup_done")
        s_rows = sem("setup_rows_identities_ready")
        s_hs = sem("setup_hi_ready")
        s_los = sem("setup_lo_ready")

        def count(it, s, n):
            return it * per_body[s.name] + max(n, 0) + 1

        def chunk(n, q):
            return CBASE[n] + q

        def fi(n):
            return FF.index(n)

        def ai(n):
            return AT.index(n)

        def glu(n, q):
            return fi(n) * C0 + q

        def plain(n, q):
            return (fi(n) - NFF // 2) * E * CH["ffn1"] + q

        def unit(n, g, u):
            return UBASE[n] + g * UNITS[kind(n)] + u

        def tile(n, g, t):
            return UBASE[n] // HG + g * TILES[kind(n)] + t

        def ends(n, q):
            per = E * CH[kind(n)] // POS
            return q // per if q % per == per - 1 else None

        def within(n, g, u):
            return {UNITS[kind(n)] // 4: 3 + 3 * g, UNITS[kind(n)] * 3 // 4 - 1: 4 + 3 * g}.get(u)

        def bank(p):
            return p if p < 4 else 2 + p % 2

        def xres(n):
            return xin[:, n % SLOTS] if n < SLOTS else xw[:, n % SLOTS]

        def flat(ap):
            return ap.rearrange("p a b -> p (a b)")

        def strip(j):
            return slice(ST * j, ST * (j + 1))

        block = ctx.enter_context(nc.Block())

        big = [(w1.rearrange("e h f -> h e f"), w1s, 0), (w3.rearrange("e h f -> h e f"), w3s, 0),
               (w2.rearrange("e (c f) d -> f (e c) d", f=P), w2s, 0)]
        for k in range(F1 // F0):
            es = slice(k * E * F0 // F1, (k + 1) * E * F0 // F1)
            big.append((W1[es].rearrange("e h f -> h e f"), W1s, k * E * F0))
            big.append((W2[es].rearrange("e (c f) d -> f (e c) d", f=P), W2s, k * E * F0))

        def row(v):
            return v.rearrange("(a n) -> a n", a=1)

        SETUP_DONE = 3

        @block.sync
        def _(sp):
            xv = x.rearrange("b (s p) d -> b p s d", p=P)
            ov = out.rearrange("b (s p) d -> b p s d", p=P)
            little = [(small[:, 0, 0], Wq), (small[:, 0, 1], Wk), (small[:, 0, 2], Wv), (small[:, 0, 3], Wo),
                      (small[:, 1, 0:3], Wqkv.rearrange("p (a b) -> p a b", b=D)), (small[:, 1, 3], Wproj),
                      (rstage[:, 0], rw0), (rstage[:, 1], Wg),
                      (b1st[:], b1.rearrange("e (c f) -> (e c) f", f=P)), (b2st[0:E], b2), (b2st[E:2 * E], b2),
                      (rows[:, 0], row(bv)), (rows[:, 1], row(bqkv[2 * D:3 * D])), (rows[:, 2], row(bo)),
                      (rows[:, 3], row(bproj)), (rows[:, 4], row(lnw)), (rows[:, 5], row(lnb)),
                      (rows[:, 6, 0:E], row(bg)), (qkrow[:, 0], row(bq)), (qkrow[:, 1], row(bk)),
                      (qkrow[:, 2], row(bqkv[0:D])), (qkrow[:, 3], row(bqkv[D:2 * D]))]
            assert len(little) == LITTLE
            for dst, src in little:
                sp.dma_start(dst, src).then_inc(s_ld, 16)
            for a in range(SLOTS):
                sp.dma_start(xin[:, a], xv[a]).then_inc(s_xin[a], 16)
            for k, (src, _, _) in enumerate(big):
                if k >= 2:
                    sp.wait_ge(s_los, k - 1)
                sp.dma_start(stage[:, k % 2].rearrange("p (a b) -> p a b", a=src.shape[1]), src)\
                  .then_inc(s_big[k % 2], 16)

            def load(it):
                for a in range(SLOTS):
                    sp.wait_ge(s_x, count(it, s_x, a + 1))
                    sp.dma_start(xin[:, a], xv[bass.ds((it + 1) * SLOTS + a, 1)].rearrange(
                        "o p s d -> p (o s) d")).then_inc(s_xin[a], 16)

            def store(it):
                for a in range(SLOTS):
                    sp.wait_ge(s_x, count(it, s_x, MAINS - SLOTS + a + 1))
                    sp.dma_start(ov[bass.ds(it * SLOTS + a, 1)].rearrange("o p s d -> p (o s) d"),
                                 xw[:, a]).then_inc(s_out, 16)

            with sp.Fori(0, BODIES - 1) as it:
                load(it)
                store(it)
            store(BODIES - 1)
            sp.wait_ge(s_out, 16 * SEQS + 1)

        @block.tensor
        def _(pe):
            mm = nc.tensor.matmul

            def product(o, weights, moving, first=True, last=True, **kw):
                terms = [(0, 0), (1, 0), (0, 1)]
                for k, (i, j) in enumerate(terms):
                    ins = mm(o, weights(i), moving(j), start=first and k == 0, stop=last and k == 2, **kw)
                return ins

            def tokens(a, j):
                return xT[:, a, j, PADL:PADL + T]

            def turn(ps, src, width, ident_, at):
                return nc.tensor.transpose(ps[:, at:at + width], src, ident_)

            pe.wait_ge(s_ld, 16 * LITTLE)
            pe.wait_ge(s_rows, 2)
            for w in range(4):
                ins = turn(U[:, 0], small[:, 0, w], P, ident[:], w * P)
            ins.then_inc(s_sp, 1)
            mm(U[:, 1], ones[:], flat(rows[:, 0:4]), start=True, stop=True)
            mm(U[:, 2, 0:2 * D + E], ones[:], flat(rows[:, 4:7])[:, 0:2 * D + E], start=True, stop=True).then_inc(s_sp, 1)
            for l in range(2):
                for k in range(2 * NG):
                    mm(U[:, 3, l * 2 * NG + k:l * 2 * NG + k + 1],
                       brow[:, l, k // NG, (k % NG) * P:(k % NG + 1) * P], ones[:, 0:1], start=True, stop=True)
            for k in range(2):
                ins = mm(U[:, 3, 4 * NG + k:4 * NG + k + 1], lrow[:, k], ones[:, 0:1], start=True, stop=True)
            ins.then_inc(s_sp, 1)
            nc.tensor.transpose(Y[:, 0, 0:E * CH["ffn1"]], b1st[:], ident[0:E * CH["ffn1"], 0:E * CH["ffn1"]])\
              .then_inc(s_sp, 1)
            pe.wait_ge(s_go, SETUP_DONE)

            def hook(it, n, pos):
                b, m = n - 1, n + 1
                if b >= 0 and is_ffn(b) and pos == 1:
                    pe.wait_ge(s_ac, count(it, s_ac, (fi(b) + 1) * E))
                    if n < MAINS and is_ffn(n):
                        pe.wait_ge(s_ct, count(it, s_ct, fi(n) + 1))
                    for s in range(NS):
                        ins = turn(T1, acc[:, b % 2, s * P:(s + 1) * P], P, ident[:], s * P)
                    ins.then_inc(s_fin, 1)
                if b >= 0 and not is_ffn(b):
                    i, l = ai(b), 0 if kind(b) == "win" else 1
                    if pos == 0:
                        pe.wait_ge(s_o, count(it, s_o, (i + 1) * NG))
                        if is_ffn(n):
                            pe.wait_ge(s_ct, count(it, s_ct, fi(n) + 1))
                        for s in range(NS):
                            ins = turn(T1, oT[:, (NG - 1) % 2, s * P:(s + 1) * P], P, ident[:], s * P)
                        ins.then_inc(s_ot, 1)
                    if pos == 2:
                        pe.wait_ge(s_ao, count(it, s_ao, (i + 1) * NG))
                        for s in range(NS):
                            ins = turn(T1, flat(ao[:, s]), P, ident[:], s * P)
                        ins.then_inc(s_at, 1)
                    if pos == 4:
                        pe.wait_ge(s_al, count(it, s_al, i + 1))
                        for s in range(NS):
                            ins = product(T1[:, s * P:(s + 1) * P], lambda i_: aT[:, i_, s * P:(s + 1) * P],
                                          lambda j: wo[:, l, j])
                        ins.then_inc(s_fin, 1)
                if m >= MAINS:
                    return
                if pos == 9:
                    pe.wait_ge(s_xn, count(it, s_xn, m + 1))
                    for s in range(NS):
                        ins = turn(T1, xn[:, m % 2, s], P, ident[:], s * P)
                    ins.then_inc(s_xt, 1)
                if pos == 11 and is_ffn(m):
                    pe.wait_ge(s_xl, count(it, s_xl, m + 1))
                    r = 0 if kind(m) == "ffn0" else 1
                    for s in range(NS):
                        at = PADL + s * P
                        ins = product(T1[:, s * E:(s + 1) * E], lambda i: xT[:, m % 2, i, at:at + P],
                                      lambda j: wr[:, r, j])
                    ins.then_inc(s_lg, 1)

            def y_read(it, n):
                if n and is_ffn(n - 1):
                    pe.wait_ge(s_yc, count(it, s_yc, (fi(n - 1) + 1) * E))
                elif n:
                    pe.wait_ge(s_o, count(it, s_o, (ai(n - 1) + 1) * NG))

            def t0_read(it, n):
                if n and is_ffn(n - 1):
                    pe.wait_ge(s_cs, count(it, s_cs, (fi(n - 1) + 1) * E))
                elif n:
                    pe.wait_ge(s_qm, count(it, s_qm, (ai(n - 1) + 1) * NG))
                    pe.wait_ge(s_ao, count(it, s_ao, (ai(n - 1) + 1) * NG - 1))

            def ffn(it, n):
                a, k = n % 2, kind(n)
                C, L, nch = CH[k], LEAD[k], E * CH[k]
                W = W1s if k == "ffn1" else w1s
                V = W2s if k == "ffn1" else w2s

                def cols(w, q):
                    return lambda i: w[:, i, q * P:(q + 1) * P]

                def gate(q):
                    if q >= 2:
                        pe.wait_ge(s_si, count(it, s_si, glu(n, q - 2) + 1))
                    product(U[:, 2 * (q % 2)], cols(w1s, q), lambda j: tokens(a, j)).then_inc(s_gt, 1)

                def up(q):
                    if k == "ffn0":
                        if q >= 2:
                            pe.wait_ge(s_pr, count(it, s_pr, glu(n, q - 2) + 1))
                        product(U[:, 2 * (q % 2) + 1], cols(w3s, q), lambda j: tokens(a, j)).then_inc(s_up, 1)
                    elif k == "ffn1":
                        if q >= 4:
                            pe.wait_ge(s_lo, count(it, s_lo, chunk(n, q - 4) + 1))
                        product(U[:, q % 4], cols(W, q), lambda j: tokens(a, j)).then_inc(s_up, 1)

                def combine():
                    pe.wait_ge(s_c2, count(it, s_c2, fi(n) + 1))
                    for s in range(NS):
                        ins = nc.tensor.transpose(T1h[0:2 * E, s * P:(s + 1) * P], c2[:, s], ident16[:])
                    ins.then_inc(s_cp, 1)

                def broadcast(e):
                    if e:
                        pe.wait_ge(s_cs, count(it, s_cs, fi(n) * E + e))
                    elif k == "ffn1":
                        pe.wait_ge(s_b2c, count(it, s_b2c, fi(n) - NFF // 2 + 1))
                    else:
                        pe.wait_ge(s_ct, count(it, s_ct, fi(n) + 1))
                        t0_read(it, n)
                    mm(T0[:], sel[:, e], cT[:, a], start=True, stop=True).then_inc(s_cb, 1)

                pe.wait_ge(s_xl, count(it, s_xl, n + 1))
                for q in range(L):
                    if k == "ffn0":
                        gate(q)
                    up(q)
                    if q == 1:
                        combine()
                y_read(it, n)
                for q in range(nch):
                    e = q // C
                    if k == "ffn0" and q + L < nch:
                        gate(q + L)
                    if q + L < nch:
                        up(q + L)
                    if k == "ffn1" and q == 1:
                        pe.wait_ge(s_ct, count(it, s_ct, fi(n) + 1))
                        t0_read(it, n)
                        mm(T0[:], b2s[:, 0], cT[:, a], start=True, stop=False)
                        mm(T0[:], b2s[:, 1], cT[:, a], start=False, stop=True).then_inc(s_b2, 1)
                    if q % C == C - 1:
                        broadcast(e)
                    if q % C == 0 and e >= 2:
                        pe.wait_ge(s_yc, count(it, s_yc, fi(n) * E + e - 1))
                    pe.wait_ge(s_lo, count(it, s_lo, chunk(n, q) + 1))
                    Q = chunk(n, q)
                    product(Y[:, e % 2], cols(V, q), lambda j: (lo if j else hi)[:, Q % 4],
                            first=q % C == 0, last=q % C == C - 1).then_inc(s_dn, 1)
                    if ends(n, q) is not None:
                        hook(it, n, ends(n, q))

            def attention(it, n):
                a, k, i = n % 2, kind(n), ai(n)
                l = 0 if k == "win" else 1
                full = k == "full"
                nu = UNITS[k]
                pe.wait_ge(s_xl, count(it, s_xl, n + 1))
                y_read(it, n)

                def project(p):
                    if p >= 4:
                        pe.wait_ge(s_pb, count(it, s_pb, i * 2 * NG + p - 1))
                    c = ((p % 2) * NG + p // 2) * P
                    product(U[:, bank(p)], lambda i_: wqk[:, l, i_, c:c + P], lambda j: tokens(a, j)).then_inc(s_pj, 1)

                for p in range(4):
                    project(p)
                for b in range(NS if full else NB):
                    at = PADL + b * P if full else b * QB
                    o = Y[:, 0, b * P:(b + 1) * P] if full else Y[:, b // HB, (b % HB) * P:(b % HB + 1) * P]
                    ins = product(o, lambda i_: xT[:, a, i_, at:at + P], lambda j: wv[:, l, j])
                ins.then_inc(s_vp, 1)
                hook(it, n, 0)
                pe.wait_ge(s_pb, count(it, s_pb, i * 2 * NG + 2))

                def for_max(g, u):
                    pe.wait_ge(s_qk, count(it, s_qk, i * 2 * NG + 2 * g + 2))
                    pe.wait_ge(s_mx, count(it, s_mx, unit(n, g, u) - 1))
                    t, h = u // HG, g * HG + u % HG
                    if full:
                        ins = mm(U[:, u % 2], q3[:, g, t * P:(t + 1) * P], kz[:, h, PADL:PADL + T],
                                 start=True, stop=True)
                    else:
                        mm(U[0:QB, u % 2, 0:HB * P], identb[:, 0:QB], flat(maskq[:, t]), start=True, stop=False)
                        for b in range(HB):
                            at = (t * HB + b) * QB
                            ins = mm(U[0:QB, u % 2, b * P:(b + 1) * P], q3[:, g, at:at + QB], kz[:, h, at:at + P],
                                     start=False, stop=b == HB - 1)
                    ins.then_inc(s_sa, 1)

                def scores(g, u):
                    pe.wait_ge(s_qm, count(it, s_qm, i * NG + g + 1))
                    pe.wait_ge(s_pe, count(it, s_pe, unit(n, g, u) - 1))
                    t, h = u // HG, g * HG + u % HG
                    if full:
                        ks = PADL + t * P
                        ins = mm(U[:, 2 + u % 2], kz[:, h, ks:ks + P], q3m[:, g % 2, 0:T], start=True, stop=True)
                    else:
                        mm(U[:, 2 + u % 2, 0:HB * QB], identb[:], flat(maskk[:, t]), start=True, stop=False)
                        for b in range(HB):
                            at = (t * HB + b) * QB
                            ins = mm(U[:, 2 + u % 2, b * QB:(b + 1) * QB], kz[:, h, at:at + P],
                                     q3m[:, g % 2, at:at + QB], start=False, stop=b == HB - 1)
                    ins.then_inc(s_sc, 1)

                def values(g, t):
                    pe.wait_ge(s_v, count(it, s_v, i + 1))
                    pe.wait_ge(s_pe, count(it, s_pe, unit(n, g, t * HG + HG)))
                    pe.wait_ge(s_o, count(it, s_o, i * NG + (g - 1 if full else g)))
                    ring = tile(n, g, t) % 2 * HG
                    for b in range(1 if full else HB):
                        for j in range(HG):
                            r, h = strip(j), g * HG + j
                            if full:
                                ins = mm(Y[r, g % 2], v4[:, t, h], pT[:, ring + j], start=t == 0,
                                         stop=t == NS - 1, tile_position=(0, ST * j))
                            else:
                                ins = mm(Y[r, t, b * QB:(b + 1) * QB], v4[:, t * HB + b, h],
                                         pT[:, ring + j, b * QB:(b + 1) * QB], start=True, stop=True,
                                         tile_position=(0, ST * j))
                    ins.then_inc(s_pv, 1)

                def turn_max(g):
                    if g == 0:
                        t0_read(it, n)
                    pe.wait_ge(s_mp, count(it, s_mp, i * NG + g + 1))
                    pe.wait_ge(s_ao, count(it, s_ao, i * NG + g - 1))
                    for b in range(NS if full else NB):
                        w = P if full else QB
                        ins = nc.tensor.transpose(T0h[:, b * w:(b + 1) * w], mp[0:w, g % 2, b], ident16[0:w, 0:w])
                    ins.then_inc(s_mt, 1)

                def turn_out(g):
                    pe.wait_ge(s_o, count(it, s_o, i * NG + g + 1))
                    pe.wait_ge(s_qm, count(it, s_qm, i * NG + min(g + 2, NG)))
                    pe.wait_ge(s_ao, count(it, s_ao, i * NG + g))
                    for s in range(NS):
                        ins = turn(T0, oT[:, g % 2, s * P:(s + 1) * P], P, ident[:], s * P)
                    ins.then_inc(s_ot, 1)

                for u in range(nu):
                    for_max(0, u)
                    if u % 2 and u < 8:
                        project(4 + u // 2)
                    if u == nu // 2 - 1:
                        hook(it, n, 1)
                turn_max(0)
                hook(it, n, 2)
                pe.wait_ge(s_pb, count(it, s_pb, (i + 1) * 2 * NG))
                for g in range(NG):
                    for u in range(nu):
                        if g + 1 < NG:
                            for_max(g + 1, u)
                        scores(g, u)
                        if u % HG == 1 and u > HG:
                            values(g, u // HG - 1)
                        if u == nu // 2 and g:
                            turn_out(g - 1)
                        if within(n, g, u) is not None:
                            hook(it, n, within(n, g, u))
                    values(g, nu // HG - 1)
                    if g + 1 < NG:
                        turn_max(g + 1)
                    hook(it, n, 5 + 3 * g)
                hook(it, n, POS - 1)

            with pe.Fori(0, BODIES) as it:
                for pos in range(POS):
                    hook(it, -1, pos)
                for n in range(MAINS):
                    (ffn if is_ffn(n) else attention)(it, n)
                hook(it, MAINS, 1)
                pe.wait_ge(s_x, count(it, s_x, MAINS))

        @block.scalar
        def _(eng):
            activate = nc.scalar.activation

            def copy(o, i, scale=1.0):
                return activate(o, i, ACT.Copy, scale=scale)

            for k, (_, dst, c) in enumerate(big):
                eng.wait_ge(s_big[k % 2], 16 * (k // 2 + 1))
                copy(dst[:, 0, c:c + E * F0], stage[:, k % 2], WS).then_inc(s_hs, 1)
            eng.sem_inc(s_go, 1)
            eng.wait_ge(s_go, SETUP_DONE)

            def hook(it, n, pos):
                b, m = n - 1, n + 1
                if b >= 0 and not is_ffn(b) and pos == 3:
                    eng.wait_ge(s_at, count(it, s_at, ai(b) + 1))
                    copy(aT[:, 0], T1[:]).then_inc(s_ah, 1)
                if m >= MAINS:
                    return
                if pos == 10:
                    eng.wait_ge(s_xt, count(it, s_xt, m + 1))
                    copy(xT[:, m % 2, 0, PADL:PADL + T], T1[:]).then_inc(s_xh, 1)
                if pos == 13 and is_ffn(m):
                    eng.wait_ge(s_ls, count(it, s_ls, fi(m) + 1))
                    activate(flat(ex[:]), flat(cw[:]), ACT.Tanh, scale=0.5).then_inc(s_ex, 1)

            def ffn(it, n):
                k, i = kind(n), fi(n)
                C, L, nch = CH[k], LEAD[k], E * CH[k]

                def silu(q):
                    eng.wait_ge(s_gt, count(it, s_gt, glu(n, q) + 1))
                    eng.wait_ge(s_pr, count(it, s_pr, glu(n, q) - 3))
                    activate(act[:, q % 4], U[:, 2 * (q % 2)], ACT.Silu, scale=1 / WS).then_inc(s_si, 1)

                def spread(e):
                    eng.wait_ge(s_yc, count(it, s_yc, i * E + e - 1))
                    eng.wait_ge(s_cb, count(it, s_cb, i * E + e + 1))
                    copy(cbs[:, e % 2], T0[:]).then_inc(s_cs, 1)

                if k == "ffn0":
                    for q in range(L):
                        silu(q)
                for q in range(nch):
                    Q = chunk(n, q)
                    eng.wait_ge(s_dn, count(it, s_dn, Q - 3))
                    if k == "ffn0":
                        eng.wait_ge(s_pr, count(it, s_pr, glu(n, q) + 1))
                        copy(hi[:, Q % 4], gated[:, Q % 4]).then_inc(s_hi, 1)
                        if q + L < nch:
                            silu(q + L)
                    else:
                        eng.wait_ge(s_up, count(it, s_up, Q + 1))
                        bias = b1c[:, q:q + 1]
                        activate(hi[:, Q % 4], U[:, q % 4], ACT.Gelu_apprx_tanh, bias=bias, scale=1 / WS)
                        activate(U[:, q % 4], U[:, q % 4], ACT.Gelu_apprx_tanh, bias=bias, scale=1 / WS)\
                            .then_inc(s_hf, 1)
                        if q == 1 + L:
                            eng.wait_ge(s_ac, count(it, s_ac, i * E))
                            eng.wait_ge(s_fin, count(it, s_fin, n - 1))
                            eng.wait_ge(s_b2, count(it, s_b2, i - NFF // 2 + 1))
                            copy(acc[:, n % 2], T0[:]).then_inc(s_b2c, 1)
                    if ends(n, q) is not None:
                        hook(it, n, ends(n, q))
                    if k == "ffn0" and q % C == C - 1:
                        spread(q // C)

            def attention(it, n):
                k, i = kind(n), ai(n)
                l = 0 if k == "win" else 1
                full = k == "full"
                nu = UNITS[k]
                w = T if full else HB * QB

                def out(g):
                    eng.wait_ge(s_pv, count(it, s_pv, tile(n, g, nu // HG)))
                    eng.wait_ge(s_ot, count(it, s_ot, i * NG + g - 1))
                    if full:
                        copy(oT[:, g % 2, 0:T], Y[:, g % 2]).then_inc(s_o, 1)
                    else:
                        copy(oT[:, g % 2].rearrange("p (a b) -> p a b", a=2), Y[:, :, 0:w]).then_inc(s_o, 1)

                def biased(p):
                    eng.wait_ge(s_pj, count(it, s_pj, i * 2 * NG + p + 1))
                    eng.wait_ge(s_qk, count(it, s_qk, i * 2 * NG + p - 1))
                    c = (p % 2) * NG + p // 2
                    bias = qkb[:, l, c:c + 1]
                    activate(qk32[:, p % 2], U[:, bank(p)], ACT.Identity, bias=bias, scale=1 / WS)
                    activate(qk16[:, p % 2], U[:, bank(p)], ACT.Identity, bias=bias, scale=1 / WS).then_inc(s_pb, 1)

                for p in range(4):
                    biased(p)
                hook(it, n, 0)
                for p in range(4, 2 * NG):
                    biased(p)
                    if p == 5:
                        hook(it, n, 1)
                hook(it, n, 2)
                for g in range(NG):
                    for u in range(nu):
                        t, j = u // HG, u % HG
                        eng.wait_ge(s_sc, count(it, s_sc, unit(n, g, u) + 1))
                        eng.wait_ge(s_pv, count(it, s_pv, tile(n, g, t) - 1))
                        activate(pT[:, tile(n, g, t) % 2 * HG + j, 0:w], U[:, 2 + u % 2, 0:w], ACT.Exp, scale=SCALE)\
                            .then_inc(s_pe, 1)
                        if u == 1 and g:
                            out(g - 1)
                        if within(n, g, u) is not None:
                            hook(it, n, within(n, g, u))
                    hook(it, n, 5 + 3 * g)
                hook(it, n, POS - 1)
                out(NG - 1)

            with eng.Fori(0, BODIES) as it:
                for pos in range(POS):
                    hook(it, -1, pos)
                for n in range(MAINS):
                    (ffn if is_ffn(n) else attention)(it, n)

        @block.gpsimd
        def _(pool):
            g = nc.gpsimd
            done = [0]

            def step(ins):
                done[0] += 1
                ins.then_inc(s_sg, 1)
                pool.wait_ge(s_sg, done[0])

            for t in (ident, ident16, identb):
                step(g.memset(t[:], 0.0))
                step(g.affine_select(out=t[:], in_=t[:], compare_op=ALU.not_equal, fill=1.0, base=0,
                                     pattern=[[-1, P]], channel_multiplier=1))
            pool.sem_inc(s_rows, 1)
            step(g.memset(sel[:], 0.0))
            for base in (0, -E):
                step(g.affine_select(out=sel[:], in_=sel[:], compare_op=ALU.not_equal, fill=1.0, base=base,
                                     pattern=[[-1, E], [0, P]], channel_multiplier=1))

            def keep(t, base, pattern, mult):
                step(g.affine_select(out=t, in_=t, compare_op=ALU.is_ge, fill=NEG, base=base, pattern=pattern,
                                     channel_multiplier=mult))

            step(g.memset(maskq[:], 0.0))
            step(g.memset(maskk[:], 0.0))
            for half in range(2):
                keep(maskq[:, half], -1, [[0, HB], [1, P]], -1)
                keep(maskq[:, half], WIN, [[0, HB], [-1, P]], 1)
                keep(maskk[:, half], -1, [[0, HB], [-1, QB]], 1)
                keep(maskk[:, half], WIN, [[0, HB], [1, QB]], -1)
            keep(maskq[:, 0, 0], -PADL, [[1, P]], 0)
            keep(maskk[:, 0, 0], -PADL, [[0, QB]], 1)
            step(g.memset(tri[:], 0.0))
            for e in range(1, E):
                step(g.memset(tri[:, e, 0:e], 1.0))
            step(g.memset(mhalf[:], -0.5))
            step(g.memset(zero[:], 0.0))
            step(g.memset(xT[:], 0.0))
            step(g.memset(q3[:], 0.0))
            step(g.memset(kz[:], 0.0))
            step(g.memset(smask[:], 1.0))
            for base, mult in ((0, 1), (ST - 1, -1)):
                step(g.affine_select(out=smask[:], in_=smask[:], compare_op=ALU.is_ge, fill=0.0, base=base,
                                     pattern=[[-mult * ST, HG]], channel_multiplier=mult))
            step(g.memset(v4[:], 0.0))
            step(g.memset(v4[:, :, :, DH:DH + 1], 1.0))
            step(g.memset(mp[:], 0.0))
            for s in loop_sems + [s_out]:
                pool.sem_inc(s, 1)
            pool.sem_inc(s_go, 1)
            pool.wait_ge(s_go, SETUP_DONE)

            def hook(it, n, pos):
                m = n + 1
                if m < MAINS and (pos == 6 or pos == 8 and kind(m) == "full"):
                    for k in [LNBASE[m] + (pos == 8)]:
                        pool.wait_ge(s_var, count(it, s_var, k + 1))
                        g.tensor_tensor(rstd[:], ve[:], mhalf[:], ALU.pow).then_inc(s_rstd, 1)

            def ffn(it, n):
                i, C = fi(n), CH[kind(n)]

                def accumulate(e):
                    if e == 0:
                        pool.wait_ge(s_fin, count(it, s_fin, n - 1))
                        if kind(n) == "ffn1":
                            pool.wait_ge(s_b2c, count(it, s_b2c, i - NFF // 2 + 1))
                    pool.wait_ge(s_yc, count(it, s_yc, i * E + e + 1))
                    if e == 0 and kind(n) == "ffn0":
                        g.tensor_tensor(acc[:, n % 2], zero[:], yc[:, e % 2], ALU.add).then_inc(s_ac, 1)
                    else:
                        pool.wait_ge(s_ac, count(it, s_ac, i * E + e))
                        g.tensor_tensor(acc[:, n % 2], acc[:, n % 2], yc[:, e % 2], ALU.add).then_inc(s_ac, 1)

                if kind(n) == "ffn0":
                    for q in range(E * C):
                        Q = chunk(n, q)
                        pool.wait_ge(s_hi, count(it, s_hi, glu(n, q) + 1))
                        g.tensor_tensor(lo[:, Q % 4], gated[:, Q % 4], hi[:, Q % 4], ALU.subtract).then_inc(s_lo, 1)
                        if q >= 2 * C + 1 and (q - 1) % C == 0:
                            accumulate((q - 1) // C - 2)
                        hook(it, n, ends(n, q))
                    accumulate(E - 2)
                    accumulate(E - 1)
                else:
                    for e in range(E):
                        accumulate(e)
                        hook(it, n, 2 * e + 2)

            with pool.Fori(0, BODIES) as it:
                hook(it, -1, 6)
                for n in range(MAINS):
                    if is_ffn(n):
                        ffn(it, n)
                    else:
                        hook(it, n, 6)
                        hook(it, n, 8)

        @block.vector
        def _(v):
            vec = nc.vector
            done = [0]

            def link(ins):
                done[0] += 1
                ins.then_inc(s_su, 1)
                v.wait_ge(s_su, done[0])

            def split(dst_hi, dst_lo, src, scale=WS):
                link(vec.tensor_scalar(dst_hi, src, scale, None, ALU.mult))
                link(vec.scalar_tensor_tensor(dst_lo, src, scale, dst_hi, ALU.mult, ALU.subtract))

            link(vec.memset(wqk[:], 0.0))
            link(vec.memset(brow, 0.0))
            link(vec.memset(lrow[:], 0.0))
            link(vec.memset(ones[:], 1.0))
            v.wait_ge(s_ld, 16 * LITTLE)
            for l in range(2):
                for k in range(2):
                    dst = brow[:, l, k].rearrange("p (h r) -> p h r", r=ST)
                    for r in range(3):
                        link(vec.tensor_copy(dst[:, :, r * DH:(r + 1) * DH],
                                             qkrow[:, 2 * l + k].rearrange("p (h d) -> p h d", d=DH)))
                link(vec.memset(brow[:, l, 1].rearrange("p (h r) -> p h r", r=ST)[:, :, MROW:MROW + 1], 1.0))
            for k, r in ((0, 2), (1, 1)):
                link(vec.memset(lrow[:, k].rearrange("p (h r) -> p h r", r=ST)[:, :, r * DH:(r + 1) * DH], -1.0))
            v.sem_inc(s_rows, 1)
            v.wait_ge(s_sp, 1)
            link(vec.tensor_copy(flat(smallT), U[:, 0]))
            for l in range(2):
                src = smallT if l == 0 else small[:, 1]
                for k in range(2):
                    w = src[:, k].rearrange("p (h d) -> p h d", d=DH)
                    at = slice(k * NG * P, (k + 1) * NG * P)
                    dst = [wqk[:, l, part, at].rearrange("p (h r) -> p h r", r=ST) for part in range(2)]
                    for r in range(3):
                        rs = slice(r * DH, (r + 1) * DH)
                        split(dst[0][:, :, rs], dst[1][:, :, rs], w)
                split(wv[:, l, 0], wv[:, l, 1], src[:, 2])
                split(wo[:, l, 0], wo[:, l, 1], src[:, 3])
                split(wr[:, l, 0], wr[:, l, 1], rstage[:, l])
            split(b2s[:, 0], b2s[:, 1], b2st[:])
            v.wait_ge(s_sp, 4)
            link(vec.tensor_copy(flat(bvb[:]), U[:, 1, 0:2 * D]))
            link(vec.tensor_copy(flat(bob[:]), U[:, 1, 2 * D:4 * D]))
            link(vec.tensor_copy(lnwb[:], U[:, 2, 0:D]))
            link(vec.tensor_copy(lnbb[:], U[:, 2, D:2 * D]))
            link(vec.tensor_copy(bgb[:], U[:, 2, 2 * D:2 * D + E]))
            link(vec.tensor_copy(flat(qkb[:]), U[:, 3, 0:4 * NG]))
            link(vec.tensor_copy(lom[:], U[:, 3, 4 * NG:4 * NG + 2]))
            link(vec.tensor_copy(b1c[:], Y[:, 0, 0:E * CH["ffn1"]]))
            for k, (_, dst, c) in enumerate(big):
                v.wait_ge(s_hs, k + 1)
                vec.scalar_tensor_tensor(dst[:, 1, c:c + E * F0], stage[:, k % 2], WS, dst[:, 0, c:c + E * F0],
                                         ALU.mult, ALU.subtract).then_inc(s_los, 1)
            v.wait_ge(s_los, len(big))
            v.sem_inc(s_go, 1)
            v.wait_ge(s_go, SETUP_DONE)
            steps = [0]

            def bcast(ap, n_, axis=2):
                shape = list(ap.shape)
                return ap.unsqueeze(axis).broadcast_to(shape[:axis] + [n_] + shape[axis:])

            def normed(it, ps, g):
                o = ps[:].rearrange("p (s j r) -> p s j r", j=HG, r=ST)
                steps[0] += 1
                vec.reciprocal(rec[:], o[:, :, :, DH]).then_inc(s_dve, 1)
                v.wait_ge(s_dve, count(it, s_dve, steps[0]))
                vec.tensor_tensor(ao[:, :, g * HG:(g + 1) * HG], o[:, :, :, 0:DH], bcast(rec[:], DH, 3),
                                  ALU.mult).then_inc(s_ao, 1)

            def hook(it, n, pos):
                m = n + 1

                def step(ins):
                    steps[0] += 1
                    ins.then_inc(s_dve, 1)
                    v.wait_ge(s_dve, count(it, s_dve, steps[0]))

                def statistics(src, tiles):
                    for s in tiles:
                        ins = vec.bn_stats(st6[:, s], src[:, s])
                    return ins

                def moments():
                    vec.memset(ve[:], 0.0)
                    for s in range(NS):
                        ins = vec.bn_aggr(mv[:, s], st6[:, s])
                    step(ins)
                    vec.tensor_scalar(ve[:], mv[:, :, 1], LN_EPS, None, ALU.add).then_inc(s_var, 1)

                def normalise(dst, src):
                    for s in range(NS):
                        ins = vec.tensor_scalar(dst[:, s], src[:, s], mv[:, s, 0:1], rstd[:, s:s + 1],
                                                ALU.subtract, ALU.mult)
                    return ins

                b = n - 1
                if b >= 0 and is_ffn(b) and pos == 2:
                    v.wait_ge(s_fin, count(it, s_fin, b + 1))
                    if b < SLOTS:
                        v.wait_ge(s_out, it * 16 * SLOTS + 1)
                    vec.scalar_tensor_tensor(flat(xw[:, b % 2]), T1[:], 0.5 / WS, flat(xres(b)), ALU.mult,
                                             ALU.add).then_inc(s_x, 1)
                if b >= 0 and not is_ffn(b):
                    i, l, res = ai(b), 0 if kind(b) == "win" else 1, xw[:, b % 2]
                    if pos == 1:
                        v.wait_ge(s_ot, count(it, s_ot, (i + 1) * NG))
                        normed(it, T1, NG - 1)
                    if pos == 3:
                        v.wait_ge(s_ah, count(it, s_ah, i + 1))
                        vec.tensor_tensor(aT[:, 1], T1[:], aT[:, 0], ALU.subtract).then_inc(s_al, 1)
                        step(vec.tensor_tensor(res, res, bcast(bob[:, l], NS, 1), ALU.add))
                    if pos == 4 and kind(b) == "full":
                        step(vec.tensor_tensor(flat(res), flat(res), flat(zz[:, b % 2]), ALU.add))
                    if pos == 5:
                        v.wait_ge(s_fin, count(it, s_fin, b + 1))
                        vec.scalar_tensor_tensor(flat(res), T1[:], 1 / WS, flat(res), ALU.mult,
                                                 ALU.add).then_inc(s_x, 1)
                if m >= MAINS:
                    return
                a = m % 2
                if pos == 5:
                    if b >= 0:
                        v.wait_ge(s_x, count(it, s_x, b + 1))
                    if m < SLOTS:
                        v.wait_ge(s_xin[a], it * 16 + 16)
                    statistics(xres(m), range(NS // 2))
                if pos == 6:
                    step(statistics(xres(m), range(NS // 2, NS)))
                    moments()
                if pos == 8:
                    v.wait_ge(s_rstd, count(it, s_rstd, LNBASE[m] + 1))
                    if kind(m) != "full":
                        normalise(xn[:, a], xres(m)).then_inc(s_xn, 1)
                    else:
                        step(normalise(zz[:, a], xres(m)))
                        step(statistics(zz[:, a], range(NS)))
                        moments()
                if pos == 9 and kind(m) == "full":
                    v.wait_ge(s_rstd, count(it, s_rstd, LNBASE[m] + 2))
                    step(normalise(xn[:, a], zz[:, a]))
                    step(vec.tensor_tensor(xn[:, a], xn[:, a], bcast(lnwb[:], NS, 1), ALU.mult))
                    vec.tensor_tensor(xn[:, a], xn[:, a], bcast(lnbb[:], NS, 1), ALU.add).then_inc(s_xn, 1)
                if pos == 11:
                    v.wait_ge(s_xh, count(it, s_xh, m + 1))
                    vec.tensor_tensor(xT[:, a, 1, PADL:PADL + T], T1[:], xT[:, a, 0, PADL:PADL + T],
                                      ALU.subtract).then_inc(s_xl, 1)
                if not is_ffn(m):
                    return
                if pos == 12:
                    v.wait_ge(s_lg, count(it, s_lg, fi(m) + 1))
                    logits = T1[:, 0:NS * E].rearrange("p (s e) -> p s e", e=E)
                    if kind(m) == "ffn0":
                        step(vec.tensor_scalar(lg[:], logits, 1 / WS, None, ALU.mult))
                    else:
                        step(vec.scalar_tensor_tensor(lg[:], logits, 1 / WS, bcast(bgb[:], NS, 1), ALU.mult,
                                                      ALU.add))
                    step(vec.tensor_reduce(mx[:], lg[:], AX, ALU.max))
                    vec.tensor_tensor(cw[:], lg[:], bcast(mx[:], E), ALU.subtract).then_inc(s_ls, 1)
                if pos == 13:
                    other, own = bcast(lg[:], E, 2), bcast(lg[:], E, 3)
                    vec.tensor_tensor(gt[:], other, own, ALU.is_gt)
                    step(vec.tensor_tensor(eq[:], other, own, ALU.is_equal))
                    step(vec.tensor_tensor(eq[:], eq[:], bcast(tri[:], NS, 1), ALU.mult))
                    step(vec.tensor_tensor(gt[:], gt[:], eq[:], ALU.add))
                    vec.tensor_reduce(rank[:], gt[:], AX, ALU.add)
                if pos == 14:
                    v.wait_ge(s_ex, count(it, s_ex, fi(m) + 1))
                    step(vec.tensor_scalar(cw[:], ex[:], -1.0, 1.0, ALU.mult, ALU.add))
                    step(vec.reciprocal(cw[:], cw[:]))
                    step(vec.scalar_tensor_tensor(flat(ex[:]), flat(ex[:]), 1.0, flat(cw[:]), ALU.add, ALU.mult))
                    step(vec.scalar_tensor_tensor(flat(cw[:]), flat(rank[:]), 1.5, flat(ex[:]), ALU.is_lt, ALU.mult))
                    step(vec.tensor_reduce(ssum[:], cw[:], AX, ALU.add))
                if pos == 15:
                    if kind(m) == "ffn1":
                        step(vec.tensor_reduce(zs[:], ex[:], AX, ALU.add))
                        step(vec.scalar_tensor_tensor(ssum[:], zs[:], 1e-8, ssum[:], ALU.mult, ALU.add))
                    step(vec.reciprocal(ssum[:], ssum[:]))
                    step(vec.tensor_tensor(cw[:], cw[:], bcast(ssum[:], E), ALU.mult))
                    step(vec.tensor_copy(c2[:, :, 0:E], cw[:]))
                    vec.tensor_tensor(c2[:, :, E:2 * E], cw[:], c2[:, :, 0:E], ALU.subtract).then_inc(s_c2, 1)

            def ffn(it, n):
                k, i = kind(n), fi(n)
                C, L, nch = CH[k], LEAD[k], E * CH[k]

                def weigh(e):
                    v.wait_ge(s_dn, count(it, s_dn, chunk(n, (e + 1) * C)))
                    v.wait_ge(s_cs, count(it, s_cs, i * E + e + 1))
                    v.wait_ge(s_ac, count(it, s_ac, i * E + e - 1))
                    vec.tensor_tensor(yc[:, e % 2], Y[:, e % 2], cbs[:, e % 2], ALU.mult).then_inc(s_yc, 1)

                def spread(e):
                    v.wait_ge(s_cb, count(it, s_cb, i * E + e + 1))
                    vec.tensor_copy(cbs[:, e % 2], T0[:]).then_inc(s_cs, 1)

                for q in range(nch):
                    Q = chunk(n, q)
                    if k == "ffn0":
                        v.wait_ge(s_si, count(it, s_si, glu(n, q) + 1))
                        v.wait_ge(s_up, count(it, s_up, Q + 1))
                        v.wait_ge(s_lo, count(it, s_lo, Q - 3))
                        vec.scalar_tensor_tensor(gated[:, Q % 4], U[:, 2 * (q % 2) + 1], 1 / WS, act[:, q % 4],
                                                 ALU.mult, ALU.mult).then_inc(s_pr, 1)
                        if q >= C + L and (q - L) % C == 0:
                            weigh((q - L) // C - 1)
                    else:
                        v.wait_ge(s_hf, count(it, s_hf, plain(n, q) + 1))
                        vec.tensor_tensor(lo[:, Q % 4], U[:, q % 4], hi[:, Q % 4], ALU.subtract).then_inc(s_lo, 1)
                        if q % C == C - 1:
                            spread(q // C)
                        if q % C == 0 and q:
                            weigh(q // C - 1)
                    if q == 0:
                        v.wait_ge(s_cp, count(it, s_cp, i + 1))
                        vec.tensor_copy(cT[:, n % 2], T1h[0:2 * E, 0:T]).then_inc(s_ct, 1)
                    if ends(n, q) is not None:
                        hook(it, n, ends(n, q))
                if k == "ffn0":
                    weigh(E - 2)
                weigh(E - 1)

            def attention(it, n):
                k, i = kind(n), ai(n)
                l = 0 if k == "win" else 1
                full = k == "full"
                nu = UNITS[k]
                nb, w, width = (NS, P, T) if full else (NB, QB, TP)

                def strips(p):
                    v.wait_ge(s_pb, count(it, s_pb, i * 2 * NG + p + 1))
                    g, hi_, exact, mask = p // 2, qk16[:, p % 2], qk32[:, p % 2], lom[:, p % 2:p % 2 + 1]
                    if p % 2 == 0:
                        vec.scalar_tensor_tensor(q3[:, g, 0:T], hi_, mask, exact, ALU.mult, ALU.add).then_inc(s_qk, 1)
                        return
                    vec.scalar_tensor_tensor(k3[:, g % 2], hi_, mask, exact, ALU.mult, ALU.add).then_inc(s_kt, 1)
                    v.wait_ge(s_kt, count(it, s_kt, i * NG + g + 1))
                    for j in range(HG):
                        ins = vec.tensor_scalar(kz[:, g * HG + j, PADL:PADL + T], k3[:, g % 2], smask[:, j:j + 1],
                                                None, ALU.mult)
                    ins.then_inc(s_qk, 1)

                for p in range(4):
                    strips(p)
                v.wait_ge(s_vp, count(it, s_vp, i + 1))
                for b in range(nb):
                    src = Y[:, 0, b * P:(b + 1) * P] if full else Y[:, b // HB, (b % HB) * P:(b % HB + 1) * P]
                    ins = vec.scalar_tensor_tensor(v4[:, b, :, 0:DH], src.rearrange("p (h d) -> p h d", d=DH), 1 / WS,
                                                   bvb[:, l].rearrange("p (h d) -> p h d", d=DH), ALU.mult, ALU.add)
                ins.then_inc(s_v, 1)
                hook(it, n, 0)

                def maxima(g, u):
                    v.wait_ge(s_sa, count(it, s_sa, unit(n, g, u) + 1))
                    t, j = u // HG, u % HG
                    if full:
                        vec.tensor_reduce(mxs[:, g % 2, j, t:t + 1], U[:, u % 2], AX, ALU.max).then_inc(s_mx, 1)
                    else:
                        vec.tensor_reduce(mxs[0:QB, g % 2, j, t * HB:(t + 1) * HB],
                                          U[0:QB, u % 2, 0:HB * P].rearrange("p (b k) -> p b k", k=P), AX,
                                          ALU.max).then_inc(s_mx, 1)

                def negate(g):
                    v.wait_ge(s_mx, count(it, s_mx, unit(n, g, nu)))
                    dst = mp[0:w, g % 2, 0:nb].rearrange("p b (j r) -> p b j r", r=ST)[:, :, :, MROW]
                    vec.tensor_scalar(dst, mxs[0:w, g % 2, :, 0:nb].rearrange("p j b -> p b j"), -1.0, None,
                                      ALU.mult).then_inc(s_mp, 1)

                def with_max(g):
                    v.wait_ge(s_mt, count(it, s_mt, i * NG + g + 1))
                    vec.tensor_tensor(q3m[:, g % 2, 0:width], T0h[:, 0:width], q3[:, g, 0:width], ALU.add)\
                        .then_inc(s_qm, 1)

                for u in range(nu):
                    maxima(0, u)
                    if u % 2 and 3 <= u <= 9:
                        strips(4 + u // 2 - 1)
                    if u == nu // 2 - 1:
                        hook(it, n, 1)
                if nu <= 9:
                    strips(2 * NG - 1)
                negate(0)
                with_max(0)
                hook(it, n, 2)
                for g in range(NG):
                    for u in range(nu):
                        if g + 1 < NG:
                            maxima(g + 1, u)
                        if within(n, g, u) is not None:
                            hook(it, n, within(n, g, u))
                    if g:
                        v.wait_ge(s_ot, count(it, s_ot, i * NG + g))
                        normed(it, T0, g - 1)
                    if g + 1 < NG:
                        negate(g + 1)
                        with_max(g + 1)
                    hook(it, n, 5 + 3 * g)
                hook(it, n, POS - 1)

            with v.Fori(0, BODIES) as it:
                for pos in range(POS):
                    hook(it, -1, pos)
                for n in range(MAINS):
                    (ffn if is_ffn(n) else attention)(it, n)
                hook(it, MAINS, 2)
            assert steps[0] == DVE_STEPS, steps[0]


_INS = ['L0_attn_x', 'L0_attn_Wq', 'L0_attn_bq', 'L0_attn_Wk', 'L0_attn_bk', 'L0_attn_Wv', 'L0_attn_bv',
        'L0_attn_Wo', 'L0_attn_bo', 'L0_ffn_router_w', 'L0_ffn_w1', 'L0_ffn_w3', 'L0_ffn_w2',
        'L1_attn_ln_w', 'L1_attn_ln_b', 'L1_attn_W_qkv', 'L1_attn_b_qkv', 'L1_attn_W_proj',
        'L1_attn_b_proj', 'L1_ffn_Wg', 'L1_ffn_bg', 'L1_ffn_W1', 'L1_ffn_b1', 'L1_ffn_W2', 'L1_ffn_b2']


def kernel(**inputs):
    import numpy as _np
    import concourse.bacc as _bacc
    from concourse import mybir as _mybir
    from concourse.bass_utils import run_bass_kernel_spmd as _run

    nc = _bacc.Bacc("TRN2", target_bir_lowering=False, num_devices=1)
    arrays, args = {}, []
    for name in _INS:
        a = _np.ascontiguousarray(inputs[name])
        arrays[f"in_{name}_dram"] = a
        args.append(nc.dram_tensor(f"in_{name}_dram", a.shape, _mybir.dt.from_np(a.dtype), kind="ExternalInput").ap())
    shape = arrays["in_L0_attn_x_dram"].shape
    args.append(nc.dram_tensor("out_0_dram", shape, _mybir.dt.float32, kind="ExternalOutput").ap())
    build(nc, *args)
    r = _run(nc, [arrays], core_ids=[0])
    return r.results[0]["out_0_dram"]
```

```python
from contextlib import ExitStack

import concourse.bass as bass
from concourse import mybir

ALU = mybir.AluOpType
ACT = mybir.ActivationFunctionType
F32 = mybir.dt.float32
F16 = mybir.dt.float16
BF16 = mybir.dt.bfloat16
AX = mybir.AxisListType.X

P = 128
D = 128
T = 512
NS = T // P
NH = 16
DH = D // NH
NG = 4
HG = NH // NG
ST = P // HG
MROW = 3 * DH
E = 8
WIN = 32
QB = P - WIN
NB = -(-T // QB)
HB = NB // 2
PADL = WIN
TP = NB * QB
TK = PADL + TP
WS = 64.0
LN_EPS = 1e-5
NEG = -1e30
SCALE = DH ** -0.5
SLOTS = 2

POS = 16
STAGES = 6
MAINS = STAGES * SLOTS
KIND = ["ffn0", "win", "ffn0", "ffn1", "full", "ffn1"]
CH = {"ffn0": 2, "ffn1": 4}
LEAD = {"ffn0": 3, "ffn1": 3}
LAG = {"ffn0": dict(act=0, pool=1, dve=2), "ffn1": dict(act=2, pool=2, dve=2)}


LATE = dict(stats=5, moments=6, norm=7, norm2=9, xT=8, xh=9, xl=10, router=11, logits=12, rank=13, tanh=13,
            weights=14, combine=15, proj0=11, bias0=12, strip0=12, proj1=13, bias1=14, strip1=14)
EARLY = dict(stats=3, moments=4, norm=6, norm2=7, xT=7, xh=8, xl=9, router=9, logits=10, rank=11, tanh=11,
             weights=12, combine=13, proj0=10, bias0=11, strip0=11, proj1=12, bias1=13, strip1=13)
FULL = dict(stats=3, moments=4, norm=5, norm2=6, xT=8, xh=9, xl=9, proj0=10, bias0=11, strip0=11, proj1=12,
            bias1=13, strip1=13)


def kind(n):
    return KIND[n // SLOTS % STAGES]


def is_ffn(n):
    return kind(n).startswith("ffn")


def hook_of(n, pos, step):
    if n + 1 < MAINS and kind(n + 1) == "full":
        return pos == FULL.get(step)
    return pos == (EARLY if n < 1 or is_ffn(n - 1) else LATE)[step]


FF = [n for n in range(MAINS) if is_ffn(n)]
AT = [n for n in range(MAINS) if not is_ffn(n)]
CBASE = [sum(E * CH[kind(m)] for m in FF if m < n) for n in range(MAINS + 1)]
LNBASE = [sum(2 if kind(m) == "full" else 1 for m in range(n)) for n in range(MAINS + 1)]
C0 = E * CH["ffn0"]
TILES = {"win": NB // HB, "full": NS}
UNITS = {k: HG * t for k, t in TILES.items()}
UBASE = [sum(NG * UNITS[kind(m)] for m in AT if m < n) for n in range(MAINS + 1)]
LATER = 7
PER_GROUP = (POS - 3 - LATER) // (NG - 1)
AHEAD = 2
LITTLE = 22
DVE_STEPS = 158


def build(nc, x, Wq, bq, Wk, bk, Wv, bv, Wo, bo, rw0, w1, w3, w2, lnw, lnb, Wqkv, bqkv, Wproj, bproj,
          Wg, bg, W1, b1, W2, b2, out):
    SEQS = x.shape[0]
    BODIES = SEQS // SLOTS
    F0, F1 = w1.shape[2], W1.shape[2]
    assert x.shape[1:] == (T, D) and F0 == CH["ffn0"] * P and F1 == CH["ffn1"] * P and SEQS % SLOTS == 0

    nc.disable_value_cache = True
    ctx = ExitStack()
    with ctx:
        def sb(name, shape, dt=F32):
            return ctx.enter_context(nc.sbuf_tensor(name, shape, dt))

        def sem(name):
            return ctx.enter_context(nc.semaphore(name))

        w1s = sb("w1s", [P, 2, E * F0], F16)
        w3s = sb("w3s", [P, 2, E * F0], F16)
        w2s = sb("w2s", [P, 2, E * F0], F16)
        W1s = sb("W1s", [P, 2, E * F1], F16)
        W2s = sb("W2s", [P, 2, E * F1], F16)
        wqk = sb("wqk", [P, 2, 2, 2 * NG * P], F16)
        wv = sb("wv", [P, 2, 2, D], F16)
        wo = sb("wo", [P, 2, 2, D], F16)
        wr = sb("wr", [P, 2, 2, E], F16)
        b2s = sb("b2s", [2 * E, 2, D], F16)
        sel = sb("sel", [2 * E, E, P], F16)
        qkb = sb("qkb", [P, 2, 2 * NG])
        lom = sb("lom", [P, 2])
        b1c = sb("b1c", [P, E * CH["ffn1"]])
        bvb = sb("bvb", [P, 2, D])
        bob = sb("bob", [P, 2, D])
        bgb = sb("bgb", [P, E])
        lnwb = sb("lnwb", [P, D])
        lnbb = sb("lnbb", [P, D])
        tri = sb("tri", [P, E, E])
        ident = sb("ident", [P, P])
        ident16 = sb("ident16", [P, P], F16)
        identb = sb("identb", [P, P], BF16)
        maskq = sb("maskq", [P, 2, HB, P], BF16)
        maskk = sb("maskk", [P, 2, HB, QB], BF16)
        mhalf = sb("mhalf", [P, NS])

        xin = sb("xin", [P, SLOTS, NS, D])
        xw = sb("xw", [P, SLOTS, NS, D])
        xn = sb("xn", [P, SLOTS, NS, D])
        zz = sb("zz", [P, SLOTS, NS, D])
        xT = sb("xT", [P, SLOTS, 2, TK], F16)
        cT = sb("cT", [2 * E, SLOTS, T], F16)
        st6 = sb("st6", [P, NS, 6])
        mv = sb("mv", [P, NS, 2])
        ve = sb("ve", [P, NS])
        rstd = sb("rstd", [P, NS])
        lg = sb("lg", [P, NS, E])
        mx = sb("mx", [P, NS])
        ex = sb("ex", [P, NS, E])
        gt = sb("gt", [P, NS, E, E])
        eq = sb("eq", [P, NS, E, E])
        rank = sb("rank", [P, NS, E])
        cw = sb("cw", [P, NS, E])
        zs = sb("zs", [P, NS])
        ssum = sb("ssum", [P, NS])
        c2 = sb("c2", [P, NS, 2 * E], F16)
        hidden = sb("hidden", [P, 2, 4, T], F16)
        hi, lo = hidden[:, 0], hidden[:, 1]
        cbs = sb("cbs", [P, 2, T])
        yc = sb("yc", [P, 2, T])
        zero = sb("zero", [P, T])
        acc = sb("acc", [P, 2, T])
        q3 = sb("q3", [P, NG, TP], F16)
        q3m = sb("q3m", [P, 2, TP], F16)
        k3 = sb("k3", [P, 2, T], F16)
        kz = sb("kz", [P, NH, TK], F16)
        smask = sb("smask", [P, HG])
        qk32 = sb("qk32", [P, 2, T])
        qk16 = sb("qk16", [P, 2, T], F16)
        v4 = sb("v4", [P, NB, NH, ST])
        mxs = sb("mxs", [P, 2, HG, NB])
        mp = sb("mp", [P, 2, NB, P], F16)
        pT = sb("pT", [P, 8, T])
        gated, act = pT[:, 0:4], pT[:, 4:8]
        oT = sb("oT", [P, 2, TP])
        rec = sb("rec", [P, NS, HG])
        ao = sb("ao", [P, NS, NH, DH])
        aT = sb("aT", [P, 2, T], F16)
        small = zz
        smallT = xn[:, 0]
        rows = acc[0:1].rearrange("p a (b d) -> p (a b) d", d=D)
        qkrow = xn[0:1, 1]
        brow = hidden[0:1].rearrange("p a b c -> p (a b c)").bitcast(F32).rearrange(
            "p (l k n) -> p l k n", l=2, k=2)
        stage = pT[:].rearrange("p (a b) c -> p a (b c)", a=2)
        rstage = sb("rstage", [P, 2, E])
        b1st = sb("b1st", [E * CH["ffn1"], P])
        b2st = sb("b2st", [2 * E, D])
        lrow = sb("lrow", [1, 2, P])
        ones = sb("ones", [1, P])

        U = ctx.enter_context(nc.psum_tensor("U", [P, 4, T], F32))
        Y = ctx.enter_context(nc.psum_tensor("Y", [P, 2, T], F32))
        T0 = ctx.enter_context(nc.psum_tensor("T0", [P, T], F32))
        T1 = ctx.enter_context(nc.psum_tensor("T1", [P, T], F32))
        T0h = T0[:].bitcast(F16)
        T1h = T1[:].bitcast(F16)

        per_body, loop_sems = {}, []

        def signal(name, times):
            s = sem(name)
            per_body[s.name] = times
            loop_sems.append(s)
            return s

        NFF, NAT = len(FF), len(AT)
        s_xin = [sem("xin_loaded0"), sem("xin_loaded1")]
        s_out = sem("out_stored")
        s_var = signal("variance_ready", LNBASE[MAINS])
        s_rstd = signal("rstd_ready", LNBASE[MAINS])
        s_xn = signal("norm_ready", MAINS)
        s_n2 = signal("second_norm_ready", SLOTS)
        s_rb = signal("residual_biased", NAT)
        s_xt = signal("normT_in_psum", MAINS)
        s_xh = signal("normT_hi_ready", MAINS)
        s_xl = signal("normT_lo_ready", MAINS)
        s_lg = signal("logits_in_psum", NFF)
        s_ls = signal("logits_shifted", NFF)
        s_ex = signal("router_exp_ready", NFF)
        s_c2 = signal("combine_ready", NFF)
        s_cp = signal("combineT_in_psum", NFF)
        s_ct = signal("combineT_ready", NFF)
        s_up = signal("up_in_psum", CBASE[MAINS])
        s_gt = signal("gate_in_psum", NFF // 2 * C0)
        s_si = signal("silu_ready", NFF // 2 * C0)
        s_pr = signal("gated_ready", NFF // 2 * C0)
        s_hi = signal("gated_hi_ready", NFF // 2 * C0)
        s_hf = signal("hidden_ready", NFF // 2 * E * CH["ffn1"])
        s_lo = signal("gated_lo_ready", NFF // 2 * C0)
        s_l1 = signal("hidden_lo_ready", NFF // 2 * E * CH["ffn1"])
        s_dn = signal("down_done", CBASE[MAINS])
        s_cb = signal("combine_bcast_in_psum", NFF * E)
        s_cs = signal("combine_bcast_ready", NFF * E)
        s_yc = signal("weighted_ready", NFF * E)
        s_ac = signal("accumulated", NFF * E)
        s_b2 = signal("bias2_in_psum", NFF // 2)
        s_b2c = signal("bias2_ready", NFF // 2)
        s_fin = signal("result_in_psum", MAINS)
        s_x = signal("residual_done", MAINS)
        s_pj = signal("proj_in_psum", NAT * 2 * NG)
        s_pb = signal("proj_biased", NAT * 2 * NG)
        s_qs = signal("q_strips_ready", NAT * NG)
        s_kt = signal("k_strips_unmasked", NAT * NG)
        s_k0 = signal("first_k_masked", NAT)
        s_kz = signal("k_masked", NAT * (NG - 1))
        s_vp = signal("v_in_psum", NAT)
        s_v = signal("v_ready", NAT)
        s_sa = signal("scores_for_max", UBASE[MAINS])
        s_mx = signal("max_taken", UBASE[MAINS])
        s_mp = signal("neg_max_ready", NAT * NG)
        s_mt = signal("neg_maxT_in_psum", NAT * NG)
        s_qm = signal("q_with_max_ready", NAT * NG)
        s_sc = signal("scores_in_psum", UBASE[MAINS])
        s_pe = signal("probs_ready", UBASE[MAINS])
        s_pv = signal("probs_used", UBASE[MAINS] // HG)
        s_o = signal("attn_outT_ready", NAT * NG)
        s_ot = signal("attn_out_in_psum", NAT * NG)
        s_ao = signal("attn_out_normed", NAT * NG)
        s_at = signal("attnT_in_psum", NAT)
        s_ah = signal("attnT_hi_ready", NAT)
        s_al = signal("attnT_lo_ready", NAT)
        s_dve = signal("vector_step", DVE_STEPS)
        s_gp = signal("gpsimd_step", 2 * SLOTS)
        s_ld = sem("weights_loaded")
        s_big = [sem("stage_loaded0"), sem("stage_loaded1")]
        s_su = sem("setup_vector_step")
        s_sg = sem("setup_gpsimd_step")
        s_sp = sem("setup_product_in_psum")
        s_go = sem("setup_done")
        s_rows = sem("setup_rows_identities_ready")
        s_hs = sem("setup_hi_ready")
        s_los = sem("setup_lo_ready")

        def count(it, s, n):
            return it * per_body[s.name] + max(n, 0) + 1

        def chunk(n, q):
            return CBASE[n] + q

        def fi(n):
            return FF.index(n) if n < MAINS else NFF

        def ai(n):
            return AT.index(n)

        def glu(n, q):
            return fi(n) * C0 + q

        def plain(n, q):
            return (fi(n) - NFF // 2) * E * CH["ffn1"] + q

        def unit(n, g, u):
            return UBASE[n] + g * UNITS[kind(n)] + u

        def tile(n, g, t):
            return UBASE[n] // HG + g * TILES[kind(n)] + t

        def ends(n, q):
            per = E * CH[kind(n)] // POS
            return q // per if q % per == per - 1 else None

        def follows(n):
            return 0 < n < MAINS and is_ffn(n - 1) and is_ffn(n)

        def behind(n, q, engine):
            k = q - LAG[kind(n)][engine]
            return ends(n, k) if 0 <= k < E * CH[kind(n)] else None

        def expert_at(n, q, lag):
            C = CH[kind(n)]
            return (q - lag) // C if 0 <= q - lag < E * C and (q - lag) % C == C - 1 else None

        def within(n, g, u):
            nu = UNITS[kind(n)]
            if g == NG - 1:
                return {nu * (k + 1) // 8 - 1: POS - LATER + k for k in range(LATER)}.get(u)
            return {nu // 4: 3 + PER_GROUP * g, nu * 3 // 4 - 1: 4 + PER_GROUP * g}.get(u)

        def beside(n, u):
            first = [2, 3, "V", 4, 5, 6, 7]
            d = 2 if kind(n) == "full" else 1
            return ([first[u // d]] if u >= 0 and u % d == d - 1 and u // d < 7 else []) + \
                ([("hook", k) for k, at in ((0, d), (1, 5 * d)) if u == at])

        def bank(p):
            return T1[:] if p < 2 else U[:, 2 + p % 2]

        def xres(n):
            return xin[:, n % SLOTS] if n % MAINS < SLOTS else xw[:, n % SLOTS]

        def flat(ap):
            return ap.rearrange("p a b -> p (a b)")

        def strip(j):
            return slice(ST * j, ST * (j + 1))

        block = ctx.enter_context(nc.Block())

        big = [(w1.rearrange("e h f -> h e f"), w1s, 0), (w3.rearrange("e h f -> h e f"), w3s, 0),
               (w2.rearrange("e (c f) d -> f (e c) d", f=P), w2s, 0)]
        for k in range(F1 // F0):
            es = slice(k * E * F0 // F1, (k + 1) * E * F0 // F1)
            big.append((W1[es].rearrange("e h f -> h e f"), W1s, k * E * F0))
            big.append((W2[es].rearrange("e (c f) d -> f (e c) d", f=P), W2s, k * E * F0))

        def row(v):
            return v.rearrange("(a n) -> a n", a=1)

        SETUP_DONE = 3

        @block.sync
        def _(sp):
            xv = x.rearrange("b (s p) d -> b p s d", p=P)
            ov = out.rearrange("b (s p) d -> b p s d", p=P)
            little = [(small[:, 0, 0], Wq), (small[:, 0, 1], Wk), (small[:, 0, 2], Wv), (small[:, 0, 3], Wo),
                      (small[:, 1, 0:3], Wqkv.rearrange("p (a b) -> p a b", b=D)), (small[:, 1, 3], Wproj),
                      (rstage[:, 0], rw0), (rstage[:, 1], Wg),
                      (b1st[:], b1.rearrange("e (c f) -> (e c) f", f=P)), (b2st[0:E], b2), (b2st[E:2 * E], b2),
                      (rows[:, 0], row(bv)), (rows[:, 1], row(bqkv[2 * D:3 * D])), (rows[:, 2], row(bo)),
                      (rows[:, 3], row(bproj)), (rows[:, 4], row(lnw)), (rows[:, 5], row(lnb)),
                      (rows[:, 6, 0:E], row(bg)), (qkrow[:, 0], row(bq)), (qkrow[:, 1], row(bk)),
                      (qkrow[:, 2], row(bqkv[0:D])), (qkrow[:, 3], row(bqkv[D:2 * D]))]
            assert len(little) == LITTLE
            for dst, src in little:
                sp.dma_start(dst, src).then_inc(s_ld, 16)
            for a in range(SLOTS):
                sp.dma_start(xin[:, a], xv[a]).then_inc(s_xin[a], 16)
            for k, (src, _, _) in enumerate(big):
                if k >= 2:
                    sp.wait_ge(s_los, k - 1)
                sp.dma_start(stage[:, k % 2].rearrange("p (a b) -> p a b", a=src.shape[1]), src)\
                  .then_inc(s_big[k % 2], 16)

            def load(it):
                for a in range(SLOTS):
                    sp.wait_ge(s_x, count(it, s_x, a + 1))
                    sp.dma_start(xin[:, a], xv[bass.ds((it + 1) * SLOTS + a, 1)].rearrange(
                        "o p s d -> p (o s) d")).then_inc(s_xin[a], 16)

            def store(it):
                for a in range(SLOTS):
                    sp.wait_ge(s_x, count(it, s_x, MAINS - SLOTS + a + 1))
                    sp.dma_start(ov[bass.ds(it * SLOTS + a, 1)].rearrange("o p s d -> p (o s) d"),
                                 xw[:, a]).then_inc(s_out, 16)

            with sp.Fori(0, BODIES - 1) as it:
                load(it)
                store(it)
            sp.wait_ge(s_x, count(BODIES - 1, s_x, 1))
            sp.dma_start(xin[:, 0], xv[0]).then_inc(s_xin[0], 16)
            store(BODIES - 1)
            sp.wait_ge(s_out, 16 * SEQS + 1)

        @block.tensor
        def _(pe):
            mm = nc.tensor.matmul

            def product(o, weights, moving, first=True, last=True, **kw):
                terms = [(0, 0), (1, 0), (0, 1)]
                for k, (i, j) in enumerate(terms):
                    ins = mm(o, weights(i), moving(j), start=first and k == 0, stop=last and k == 2, **kw)
                return ins

            def tokens(a, j):
                return xT[:, a, j, PADL:PADL + T]

            def turn(ps, src, width, ident_, at):
                return nc.tensor.transpose(ps[:, at:at + width], src, ident_)

            pe.wait_ge(s_ld, 16 * LITTLE)
            pe.wait_ge(s_rows, 2)
            for w in range(4):
                ins = turn(U[:, 0], small[:, 0, w], P, ident[:], w * P)
            ins.then_inc(s_sp, 1)
            mm(U[:, 1], ones[:], flat(rows[:, 0:4]), start=True, stop=True)
            mm(U[:, 2, 0:2 * D + E], ones[:], flat(rows[:, 4:7])[:, 0:2 * D + E], start=True, stop=True).then_inc(s_sp, 1)
            for l in range(2):
                for k in range(2 * NG):
                    mm(U[:, 3, l * 2 * NG + k:l * 2 * NG + k + 1],
                       brow[:, l, k // NG, (k % NG) * P:(k % NG + 1) * P], ones[:, 0:1], start=True, stop=True)
            for k in range(2):
                ins = mm(U[:, 3, 4 * NG + k:4 * NG + k + 1], lrow[:, k], ones[:, 0:1], start=True, stop=True)
            ins.then_inc(s_sp, 1)
            nc.tensor.transpose(Y[:, 0, 0:E * CH["ffn1"]], b1st[:], ident[0:E * CH["ffn1"], 0:E * CH["ffn1"]])\
              .then_inc(s_sp, 1)
            pe.wait_ge(s_go, SETUP_DONE)

            def hook(it, n, pos):
                b, m = n - 1, n + 1
                if b >= 0 and is_ffn(b) and pos == 2:
                    pe.wait_ge(s_ac, count(it, s_ac, (fi(b) + 1) * E))
                    if n < MAINS and is_ffn(n):
                        pe.wait_ge(s_ct, count(it, s_ct, fi(n) + 1))
                    elif n < MAINS:
                        pe.wait_ge(s_pb, count(it, s_pb, ai(n) * 2 * NG + 2))
                    else:
                        pe.wait_ge(s_ls, count(it, s_ls, NFF + 1))
                    for s in range(NS):
                        ins = turn(T1, acc[:, b % 2, s * P:(s + 1) * P], P, ident[:], s * P)
                    ins.then_inc(s_fin, 1)
                if b >= 0 and not is_ffn(b):
                    i, l = ai(b), 0 if kind(b) == "win" else 1
                    if pos == 0:
                        pe.wait_ge(s_o, count(it, s_o, (i + 1) * NG))
                        if is_ffn(n):
                            pe.wait_ge(s_ct, count(it, s_ct, fi(n) + 1))
                        else:
                            pe.wait_ge(s_pb, count(it, s_pb, ai(n) * 2 * NG + 2))
                        for s in range(NS):
                            ins = turn(T1, oT[:, (NG - 1) % 2, s * P:(s + 1) * P], P, ident[:], s * P)
                        ins.then_inc(s_ot, 1)
                    if pos == 2:
                        pe.wait_ge(s_ao, count(it, s_ao, (i + 1) * NG))
                        for s in range(NS):
                            ins = turn(T1, flat(ao[:, s]), P, ident[:], s * P)
                        ins.then_inc(s_at, 1)
                    if pos == 4:
                        pe.wait_ge(s_al, count(it, s_al, i + 1))
                        for s in range(NS):
                            ins = product(T1[:, s * P:(s + 1) * P], lambda i_: aT[:, i_, s * P:(s + 1) * P],
                                          lambda j: wo[:, l, j])
                        ins.then_inc(s_fin, 1)
                if m > MAINS:
                    return
                if hook_of(n, pos, "xT"):
                    pe.wait_ge(s_xn, count(it, s_xn, m + 1))
                    for s in range(NS):
                        ins = turn(T1, xn[:, m % 2, s], P, ident[:], s * P)
                    ins.then_inc(s_xt, 1)
                if hook_of(n, pos, "router") and is_ffn(m):
                    pe.wait_ge(s_xl, count(it, s_xl, m + 1))
                    r = 0 if kind(m) == "ffn0" else 1
                    for s in range(NS):
                        at = PADL + s * P
                        ins = product(T1[:, s * E:(s + 1) * E], lambda i: xT[:, m % 2, i, at:at + P],
                                      lambda j: wr[:, r, j])
                    ins.then_inc(s_lg, 1)
                if hook_of(n, pos, "proj0") and not is_ffn(m):
                    pe.wait_ge(s_xl, count(it, s_xl, m + 1))
                    project(m, 0).then_inc(s_pj, 1)
                if hook_of(n, pos, "proj1") and not is_ffn(m):
                    pe.wait_ge(s_pb, count(it, s_pb, ai(m) * 2 * NG + 1))
                    project(m, 1).then_inc(s_pj, 1)

            def project(n, p):
                l, c = 0 if kind(n) == "win" else 1, ((p % 2) * NG + p // 2) * P
                return product(bank(p), lambda i_: wqk[:, l, i_, c:c + P], lambda j: tokens(n % 2, j))

            def y_read(it, n):
                if n and is_ffn(n - 1):
                    pe.wait_ge(s_yc, count(it, s_yc, (fi(n - 1) + 1) * E))
                elif n:
                    pe.wait_ge(s_o, count(it, s_o, (ai(n - 1) + 1) * NG))

            def t0_read(it, n):
                if n and is_ffn(n - 1):
                    pe.wait_ge(s_cs, count(it, s_cs, (fi(n - 1) + 1) * E))
                elif n:
                    pe.wait_ge(s_qm, count(it, s_qm, (ai(n - 1) + 1) * NG))
                    pe.wait_ge(s_ao, count(it, s_ao, (ai(n - 1) + 1) * NG - 1))

            def ffn(it, n):
                a, k = n % 2, kind(n)
                C, L, nch = CH[k], LEAD[k], E * CH[k]
                V = W2s if k == "ffn1" else w2s

                def cols(w, q):
                    return lambda i: w[:, i, q * P:(q + 1) * P]

                def ahead(m, q):
                    b, j = m % 2, q % 2
                    if kind(m) == "ffn0":
                        if q >= 2 or follows(m):
                            pe.wait_ge(s_si, count(it, s_si, glu(m, q) - 1))
                        product(U[:, 2 * j], cols(w1s, q), lambda i: tokens(b, i)).then_inc(s_gt, 1)
                        if q >= 2 or follows(m):
                            pe.wait_ge(s_pr, count(it, s_pr, glu(m, q) - 1))
                        product(U[:, 2 * j + 1], cols(w3s, q), lambda i: tokens(b, i)).then_inc(s_up, 1)
                        return
                    if q >= 4 or follows(m) and kind(m - 1) == "ffn1":
                        pe.wait_ge(s_l1, count(it, s_l1, plain(m, q) - 3))
                    elif follows(m):
                        pe.wait_ge(s_pr, count(it, s_pr, glu(m, 0) - 1 + q // 2))
                    product(U[:, q % 4], cols(W1s, q), lambda i: tokens(b, i)).then_inc(s_up, 1)

                def combine():
                    pe.wait_ge(s_c2, count(it, s_c2, fi(n) + 1))
                    for s in range(NS):
                        ins = nc.tensor.transpose(T1h[0:2 * E, s * P:(s + 1) * P], c2[:, s], ident16[:])
                    ins.then_inc(s_cp, 1)

                def broadcast(e):
                    if e:
                        pe.wait_ge(s_cs, count(it, s_cs, fi(n) * E + e))
                    elif k == "ffn1":
                        pe.wait_ge(s_b2c, count(it, s_b2c, fi(n) - NFF // 2 + 1))
                    else:
                        pe.wait_ge(s_ct, count(it, s_ct, fi(n) + 1))
                        t0_read(it, n)
                    mm(T0[:], sel[:, e], cT[:, a], start=True, stop=True).then_inc(s_cb, 1)

                if not follows(n):
                    pe.wait_ge(s_xl, count(it, s_xl, n + 1))
                    for q in range(L):
                        ahead(n, q)
                    combine()
                    y_read(it, n)
                for q in range(nch):
                    e = q // C
                    if q + L < nch:
                        ahead(n, q + L)
                    elif follows(n + 1):
                        if q + L == nch:
                            pe.wait_ge(s_xl, count(it, s_xl, n + 2))
                        ahead(n + 1, q + L - nch)
                    if q == 1 and follows(n):
                        combine()
                    if k == "ffn1" and q == 2:
                        pe.wait_ge(s_ct, count(it, s_ct, fi(n) + 1))
                        t0_read(it, n)
                        mm(T0[:], b2s[:, 0], cT[:, a], start=True, stop=False)
                        mm(T0[:], b2s[:, 1], cT[:, a], start=False, stop=True).then_inc(s_b2, 1)
                    if q % C == 0 and (e >= 2 or follows(n)):
                        pe.wait_ge(s_yc, count(it, s_yc, fi(n) * E + e - 1))
                    if k == "ffn0":
                        pe.wait_ge(s_lo, count(it, s_lo, glu(n, q) + 1))
                    else:
                        pe.wait_ge(s_l1, count(it, s_l1, plain(n, q) + 1))
                    Q = chunk(n, q)
                    product(Y[:, e % 2], cols(V, q), lambda j: (lo if j else hi)[:, Q % 4],
                            first=q % C == 0, last=q % C == C - 1).then_inc(s_dn, 1)
                    if q % C == C - 1:
                        broadcast(e)
                    if ends(n, q) is not None:
                        hook(it, n, ends(n, q))

            def attention(it, n):
                a, k, i = n % 2, kind(n), ai(n)
                l = 0 if k == "win" else 1
                full = k == "full"
                nu = UNITS[k]

                def keep_v():
                    y_read(it, n)
                    for b in range(NS if full else NB):
                        at = PADL + b * P if full else b * QB
                        o = Y[:, 0, b * P:(b + 1) * P] if full else Y[:, b // HB, (b % HB) * P:(b % HB + 1) * P]
                        ins = product(o, lambda i_: xT[:, a, i_, at:at + P], lambda j: wv[:, l, j])
                    ins.then_inc(s_vp, 1)

                def for_max(g, u):
                    pe.wait_ge(s_qs, count(it, s_qs, i * NG + g + 1))
                    if g == 0:
                        pe.wait_ge(s_k0, count(it, s_k0, i + 1))
                    else:
                        pe.wait_ge(s_kz, count(it, s_kz, i * (NG - 1) + g))
                    pe.wait_ge(s_mx, count(it, s_mx, unit(n, g, u) - 1))
                    t, h = u // HG, g * HG + u % HG
                    if full:
                        ins = mm(U[:, u % 2], q3[:, g, t * P:(t + 1) * P], kz[:, h, PADL:PADL + T],
                                 start=True, stop=True)
                    else:
                        mm(U[0:QB, u % 2, 0:HB * P], identb[:, 0:QB], flat(maskq[:, t]), start=True, stop=False)
                        for b in range(HB):
                            at = (t * HB + b) * QB
                            ins = mm(U[0:QB, u % 2, b * P:(b + 1) * P], q3[:, g, at:at + QB], kz[:, h, at:at + P],
                                     start=False, stop=b == HB - 1)
                    ins.then_inc(s_sa, 1)

                def scores(g, u):
                    pe.wait_ge(s_qm, count(it, s_qm, i * NG + g + 1))
                    pe.wait_ge(s_pe, count(it, s_pe, unit(n, g, u) - 1))
                    t, h = u // HG, g * HG + u % HG
                    if full:
                        ks = PADL + t * P
                        ins = mm(U[:, 2 + u % 2], kz[:, h, ks:ks + P], q3m[:, g % 2, 0:T], start=True, stop=True)
                    else:
                        mm(U[:, 2 + u % 2, 0:HB * QB], identb[:], flat(maskk[:, t]), start=True, stop=False)
                        for b in range(HB):
                            at = (t * HB + b) * QB
                            ins = mm(U[:, 2 + u % 2, b * QB:(b + 1) * QB], kz[:, h, at:at + P],
                                     q3m[:, g % 2, at:at + QB], start=False, stop=b == HB - 1)
                    ins.then_inc(s_sc, 1)

                def values(g, t):
                    pe.wait_ge(s_v, count(it, s_v, i + 1))
                    pe.wait_ge(s_pe, count(it, s_pe, unit(n, g, t * HG + HG)))
                    pe.wait_ge(s_o, count(it, s_o, i * NG + (g - 1 if full else g)))
                    ring = tile(n, g, t) % 2 * HG
                    for b in range(1 if full else HB):
                        for j in range(HG):
                            r, h = strip(j), g * HG + j
                            if full:
                                ins = mm(Y[r, g % 2], v4[:, t, h], pT[:, ring + j], start=t == 0,
                                         stop=t == NS - 1, tile_position=(0, ST * j))
                            else:
                                ins = mm(Y[r, t, b * QB:(b + 1) * QB], v4[:, t * HB + b, h],
                                         pT[:, ring + j, b * QB:(b + 1) * QB], start=True, stop=True,
                                         tile_position=(0, ST * j))
                    ins.then_inc(s_pv, 1)

                def turn_max(g):
                    if g == 0:
                        t0_read(it, n)
                    pe.wait_ge(s_mp, count(it, s_mp, i * NG + g + 1))
                    pe.wait_ge(s_ao, count(it, s_ao, i * NG + g - 1))
                    for b in range(NS if full else NB):
                        w = P if full else QB
                        ins = nc.tensor.transpose(T0h[:, b * w:(b + 1) * w], mp[0:w, g % 2, b], ident16[0:w, 0:w])
                    ins.then_inc(s_mt, 1)

                def turn_out(g):
                    pe.wait_ge(s_o, count(it, s_o, i * NG + g + 1))
                    pe.wait_ge(s_qm, count(it, s_qm, i * NG + min(g + 2, NG)))
                    pe.wait_ge(s_ao, count(it, s_ao, i * NG + g))
                    for s in range(NS):
                        ins = turn(T0, oT[:, g % 2, s * P:(s + 1) * P], P, ident[:], s * P)
                    ins.then_inc(s_ot, 1)

                for u in range(nu):
                    for_max(0, u)
                    for what in beside(n, u):
                        if what == "V":
                            keep_v()
                        elif type(what) is tuple:
                            hook(it, n, what[1])
                        else:
                            if what == 2 and not is_ffn(n - 1):
                                pe.wait_ge(s_pe, count(it, s_pe, UBASE[n]))
                            if what >= 4:
                                pe.wait_ge(s_pb, count(it, s_pb, i * 2 * NG + what - 1))
                            project(n, what).then_inc(s_pj, 1)
                for_max(1, 0)
                turn_max(0)
                for_max(1, 1)
                hook(it, n, 2)
                pe.wait_ge(s_pb, count(it, s_pb, (i + 1) * 2 * NG))
                for g in range(NG):
                    for u in range(nu):
                        if g + 1 + (u + AHEAD) // nu < NG:
                            for_max(g + 1 + (u + AHEAD) // nu, (u + AHEAD) % nu)
                        scores(g, u)
                        if u == nu - AHEAD and g + 1 < NG:
                            turn_max(g + 1)
                        if u % HG == 1 and u > HG:
                            values(g, u // HG - 1)
                        if u == nu // 2 and g:
                            turn_out(g - 1)
                        if within(n, g, u) is not None:
                            hook(it, n, within(n, g, u))
                    values(g, nu // HG - 1)

            for pos in range(POS):
                hook(0, -1, pos)
            with pe.Fori(0, BODIES) as it:
                for n in range(MAINS):
                    (ffn if is_ffn(n) else attention)(it, n)
                hook(it, MAINS, 2)
                pe.wait_ge(s_x, count(it, s_x, MAINS))

        @block.scalar
        def _(eng):
            activate = nc.scalar.activation

            def copy(o, i, scale=1.0):
                return activate(o, i, ACT.Copy, scale=scale)

            for k, (_, dst, c) in enumerate(big):
                eng.wait_ge(s_big[k % 2], 16 * (k // 2 + 1))
                copy(dst[:, 0, c:c + E * F0], stage[:, k % 2], WS).then_inc(s_hs, 1)
            eng.sem_inc(s_go, 1)
            eng.wait_ge(s_go, SETUP_DONE)

            def hook(it, n, pos):
                b, m = n - 1, n + 1
                if b >= 0 and not is_ffn(b) and pos == 3:
                    eng.wait_ge(s_at, count(it, s_at, ai(b) + 1))
                    copy(aT[:, 0], T1[:]).then_inc(s_ah, 1)
                if m > MAINS:
                    return
                if hook_of(n, pos, "xh"):
                    eng.wait_ge(s_xt, count(it, s_xt, m + 1))
                    copy(xT[:, m % 2, 0, PADL:PADL + T], T1[:]).then_inc(s_xh, 1)
                if hook_of(n, pos, "tanh") and is_ffn(m):
                    eng.wait_ge(s_ls, count(it, s_ls, fi(m) + 1))
                    activate(flat(ex[:]), flat(cw[:]), ACT.Tanh, scale=0.5).then_inc(s_ex, 1)
                for p in range(2):
                    if hook_of(n, pos, "bias%d" % p) and not is_ffn(m):
                        biased(it, m, p)

            def biased(it, n, p):
                i, l = ai(n), 0 if kind(n) == "win" else 1
                eng.wait_ge(s_pj, count(it, s_pj, i * 2 * NG + p + 1))
                if p % 2 == 0:
                    eng.wait_ge(s_qs, count(it, s_qs, i * NG + p // 2))
                else:
                    eng.wait_ge(s_kt, count(it, s_kt, i * NG + p // 2))
                c = (p % 2) * NG + p // 2
                bias = qkb[:, l, c:c + 1]
                activate(qk32[:, p % 2], bank(p), ACT.Identity, bias=bias, scale=1 / WS)
                activate(qk16[:, p % 2], bank(p), ACT.Identity, bias=bias, scale=1 / WS).then_inc(s_pb, 1)

            def ffn(it, n):
                k, i = kind(n), fi(n)
                C, L, nch = CH[k], LEAD[k], E * CH[k]

                def silu(m, q):
                    eng.wait_ge(s_gt, count(it, s_gt, glu(m, q) + 1))
                    eng.wait_ge(s_pr, count(it, s_pr, glu(m, q) - 3))
                    activate(act[:, q % 4], U[:, 2 * (q % 2)], ACT.Silu, scale=1 / WS).then_inc(s_si, 1)

                def spread(i, e):
                    eng.wait_ge(s_yc, count(it, s_yc, i * E + e - 1))
                    eng.wait_ge(s_cb, count(it, s_cb, i * E + e + 1))
                    copy(cbs[:, e % 2], T0[:]).then_inc(s_cs, 1)

                if k == "ffn0" and not follows(n):
                    for q in range(L):
                        silu(n, q)
                lag = LAG[k]["act"]
                for q in range(nch + max(lag, 0 if follows(n + 1) else 1)):
                    Q = chunk(n, q)
                    if q < nch:
                        eng.wait_ge(s_dn, count(it, s_dn, Q - 3))
                        if k == "ffn0":
                            eng.wait_ge(s_pr, count(it, s_pr, glu(n, q) + 1))
                            copy(hi[:, Q % 4], gated[:, Q % 4]).then_inc(s_hi, 1)
                            if q + L < nch:
                                silu(n, q + L)
                            elif follows(n + 1) and kind(n + 1) == k:
                                silu(n + 1, q + L - nch)
                        else:
                            eng.wait_ge(s_up, count(it, s_up, Q + 1))
                            bias = b1c[:, q:q + 1]
                            activate(hi[:, Q % 4], U[:, q % 4], ACT.Gelu_apprx_tanh, bias=bias, scale=1 / WS)
                            activate(U[:, q % 4], U[:, q % 4], ACT.Gelu_apprx_tanh, bias=bias, scale=1 / WS)\
                                .then_inc(s_hf, 1)
                            if q == 2 + L:
                                eng.wait_ge(s_fin, count(it, s_fin, n - 1))
                                eng.wait_ge(s_b2, count(it, s_b2, i - NFF // 2 + 1))
                                copy(acc[:, n % 2], T0[:]).then_inc(s_b2c, 1)
                    if k == "ffn0" and expert_at(n, q, 1) is not None:
                        spread(i, expert_at(n, q, 1))
                    if q == 0 and follows(n) and kind(n - 1) == "ffn0":
                        spread(i - 1, E - 1)
                    if behind(n, q, "act") is not None:
                        hook(it, n, behind(n, q, "act"))

            def attention(it, n):
                k, i = kind(n), ai(n)
                l = 0 if k == "win" else 1
                full = k == "full"
                nu = UNITS[k]
                w = T if full else HB * QB

                def out(g):
                    eng.wait_ge(s_pv, count(it, s_pv, tile(n, g, nu // HG)))
                    eng.wait_ge(s_ot, count(it, s_ot, i * NG + g - 1))
                    if full:
                        copy(oT[:, g % 2, 0:T], Y[:, g % 2]).then_inc(s_o, 1)
                    else:
                        copy(oT[:, g % 2].rearrange("p (a b) -> p a b", a=2), Y[:, :, 0:w]).then_inc(s_o, 1)

                for u in range(nu):
                    for what in beside(n, u):
                        if type(what) is tuple:
                            hook(it, n, what[1])
                        elif what != "V":
                            biased(it, n, what)
                hook(it, n, 2)
                for g in range(NG):
                    for u in range(nu):
                        t, j = u // HG, u % HG
                        eng.wait_ge(s_sc, count(it, s_sc, unit(n, g, u) + 1))
                        eng.wait_ge(s_pv, count(it, s_pv, tile(n, g, t) - 1))
                        activate(pT[:, tile(n, g, t) % 2 * HG + j, 0:w], U[:, 2 + u % 2, 0:w], ACT.Exp, scale=SCALE)\
                            .then_inc(s_pe, 1)
                        if u == 1 and g:
                            out(g - 1)
                        if within(n, g, u) is not None:
                            hook(it, n, within(n, g, u))
                out(NG - 1)

            for pos in range(POS):
                hook(0, -1, pos)
            with eng.Fori(0, BODIES) as it:
                for n in range(MAINS):
                    (ffn if is_ffn(n) else attention)(it, n)

        @block.gpsimd
        def _(pool):
            g = nc.gpsimd
            done = [0]

            def step(ins):
                done[0] += 1
                ins.then_inc(s_sg, 1)
                pool.wait_ge(s_sg, done[0])

            for t in (ident, ident16, identb):
                step(g.memset(t[:], 0.0))
                step(g.affine_select(out=t[:], in_=t[:], compare_op=ALU.not_equal, fill=1.0, base=0,
                                     pattern=[[-1, P]], channel_multiplier=1))
            pool.sem_inc(s_rows, 1)
            step(g.memset(sel[:], 0.0))
            for base in (0, -E):
                step(g.affine_select(out=sel[:], in_=sel[:], compare_op=ALU.not_equal, fill=1.0, base=base,
                                     pattern=[[-1, E], [0, P]], channel_multiplier=1))

            def keep(t, base, pattern, mult):
                step(g.affine_select(out=t, in_=t, compare_op=ALU.is_ge, fill=NEG, base=base, pattern=pattern,
                                     channel_multiplier=mult))

            step(g.memset(maskq[:], 0.0))
            step(g.memset(maskk[:], 0.0))
            for half in range(2):
                keep(maskq[:, half], -1, [[0, HB], [1, P]], -1)
                keep(maskq[:, half], WIN, [[0, HB], [-1, P]], 1)
                keep(maskk[:, half], -1, [[0, HB], [-1, QB]], 1)
                keep(maskk[:, half], WIN, [[0, HB], [1, QB]], -1)
            keep(maskq[:, 0, 0], -PADL, [[1, P]], 0)
            keep(maskk[:, 0, 0], -PADL, [[0, QB]], 1)
            step(g.memset(tri[:], 0.0))
            for e in range(1, E):
                step(g.memset(tri[:, e, 0:e], 1.0))
            step(g.memset(mhalf[:], -0.5))
            step(g.memset(zero[:], 0.0))
            step(g.memset(xT[:], 0.0))
            step(g.memset(q3[:], 0.0))
            step(g.memset(kz[:], 0.0))
            step(g.memset(smask[:], 1.0))
            for base, mult in ((0, 1), (ST - 1, -1)):
                step(g.affine_select(out=smask[:], in_=smask[:], compare_op=ALU.is_ge, fill=0.0, base=base,
                                     pattern=[[-mult * ST, HG]], channel_multiplier=mult))
            step(g.memset(v4[:], 0.0))
            step(g.memset(v4[:, :, :, DH:DH + 1], 1.0))
            step(g.memset(mp[:], 0.0))
            for s in loop_sems + [s_out]:
                pool.sem_inc(s, 1)
            pool.sem_inc(s_go, 1)
            pool.wait_ge(s_go, SETUP_DONE)
            steps = [0]

            def tiles(ap):
                return ap.unsqueeze(1).broadcast_to([P, NS, D])

            def ordered(it, ins):
                steps[0] += 1
                ins.then_inc(s_gp, 1)
                pool.wait_ge(s_gp, count(it, s_gp, steps[0]))

            def hook(it, n, pos):
                m, b = n + 1, n - 1
                if pos == 3 and b >= 0 and not is_ffn(b):
                    res, full = xw[:, b % 2], kind(b) == "full"
                    pool.wait_ge(s_xn, count(it, s_xn, b + 1))
                    ins = g.tensor_tensor(res, res, tiles(bob[:, 1 if full else 0]), ALU.add)
                    if full:
                        ordered(it, ins)
                        ins = g.tensor_tensor(res, res, zz[:, b % 2], ALU.add)
                    ins.then_inc(s_rb, 1)
                if m > MAINS:
                    return
                if hook_of(n, pos, "norm2") and kind(m) == "full":
                    pool.wait_ge(s_n2, count(it, s_n2, m % 2 + 1))
                    ordered(it, g.tensor_tensor(xn[:, m % 2], xn[:, m % 2], tiles(lnwb[:]), ALU.mult))
                    g.tensor_tensor(xn[:, m % 2], xn[:, m % 2], tiles(lnbb[:]), ALU.add).then_inc(s_xn, 1)
                if hook_of(n, pos, "moments"):
                    pool.wait_ge(s_var, count(it, s_var, LNBASE[m] + 1))
                    g.tensor_tensor(rstd[:], ve[:], mhalf[:], ALU.pow).then_inc(s_rstd, 1)
                if hook_of(n, pos, "norm") and kind(m) == "full":
                    pool.wait_ge(s_var, count(it, s_var, LNBASE[m] + 2))
                    g.tensor_tensor(rstd[:], ve[:], mhalf[:], ALU.pow).then_inc(s_rstd, 1)

            def accumulate(it, n, e):
                i = fi(n)
                if e == 0:
                    pool.wait_ge(s_fin, count(it, s_fin, n - 1))
                    if kind(n) == "ffn1":
                        pool.wait_ge(s_b2c, count(it, s_b2c, i - NFF // 2 + 1))
                pool.wait_ge(s_yc, count(it, s_yc, i * E + e + 1))
                if e == 0 and kind(n) == "ffn0":
                    g.tensor_tensor(acc[:, n % 2], zero[:], yc[:, e % 2], ALU.add).then_inc(s_ac, 1)
                else:
                    pool.wait_ge(s_ac, count(it, s_ac, i * E + e))
                    g.tensor_tensor(acc[:, n % 2], acc[:, n % 2], yc[:, e % 2], ALU.add).then_inc(s_ac, 1)

            def beside_chunk(it, n, q):
                if expert_at(n, q, LEAD["ffn0"] + 1) is not None:
                    accumulate(it, n, expert_at(n, q, LEAD["ffn0"] + 1))
                if behind(n, q, "pool") is not None:
                    hook(it, n, behind(n, q, "pool"))

            def ffn(it, n):
                nch, tail = E * CH["ffn0"], LEAD["ffn0"] + 1
                last = n - 1 if follows(n) and kind(n - 1) == "ffn0" else None
                if kind(n) == "ffn0":
                    for q in range(nch):
                        Q = chunk(n, q)
                        pool.wait_ge(s_hi, count(it, s_hi, glu(n, q) + 1))
                        g.tensor_tensor(lo[:, Q % 4], gated[:, Q % 4], hi[:, Q % 4], ALU.subtract).then_inc(s_lo, 1)
                        if last is not None and q < tail:
                            beside_chunk(it, last, nch + q)
                        beside_chunk(it, n, q)
                elif last is not None:
                    for q in range(tail):
                        beside_chunk(it, last, nch + q)
                if kind(n) == "ffn0":
                    if not follows(n + 1):
                        for q in range(tail):
                            beside_chunk(it, n, nch + q)
                else:
                    for pos in range(2):
                        hook(it, n, pos)
                    for e in range(E):
                        for pos in (2 * e + 2, 2 * e + 3):
                            hook(it, n, pos)
                        accumulate(it, n, e)

            def attention(it, n):
                i = ai(n)
                for grp in range(1, NG):
                    pool.wait_ge(s_kt, count(it, s_kt, i * NG + grp + 1))
                    for j in range(HG):
                        ins = g.tensor_tensor(kz[:, grp * HG + j, PADL:PADL + T], k3[:, grp % 2],
                                              smask[:, j:j + 1].broadcast_to([P, T]), ALU.mult)
                    ins.then_inc(s_kz, 1)
                for pos in range(POS):
                    hook(it, n, pos)

            for pos in range(POS):
                hook(0, -1, pos)
            with pool.Fori(0, BODIES) as it:
                for n in range(MAINS):
                    (ffn if is_ffn(n) else attention)(it, n)
            assert steps[0] == per_body[s_gp.name]

        @block.vector
        def _(v):
            vec = nc.vector
            done = [0]

            def link(ins):
                done[0] += 1
                ins.then_inc(s_su, 1)
                v.wait_ge(s_su, done[0])

            def split(dst_hi, dst_lo, src, scale=WS):
                link(vec.tensor_scalar(dst_hi, src, scale, None, ALU.mult))
                link(vec.scalar_tensor_tensor(dst_lo, src, scale, dst_hi, ALU.mult, ALU.subtract))

            link(vec.memset(wqk[:], 0.0))
            link(vec.memset(brow, 0.0))
            link(vec.memset(lrow[:], 0.0))
            link(vec.memset(ones[:], 1.0))
            v.wait_ge(s_ld, 16 * LITTLE)
            for l in range(2):
                for k in range(2):
                    dst = brow[:, l, k].rearrange("p (h r) -> p h r", r=ST)
                    for r in range(3):
                        link(vec.tensor_copy(dst[:, :, r * DH:(r + 1) * DH],
                                             qkrow[:, 2 * l + k].rearrange("p (h d) -> p h d", d=DH)))
                link(vec.memset(brow[:, l, 1].rearrange("p (h r) -> p h r", r=ST)[:, :, MROW:MROW + 1], 1.0))
            for k, r in ((0, 2), (1, 1)):
                link(vec.memset(lrow[:, k].rearrange("p (h r) -> p h r", r=ST)[:, :, r * DH:(r + 1) * DH], -1.0))
            v.sem_inc(s_rows, 1)
            v.wait_ge(s_sp, 1)
            link(vec.tensor_copy(flat(smallT), U[:, 0]))
            for l in range(2):
                src = smallT if l == 0 else small[:, 1]
                for k in range(2):
                    w = src[:, k].rearrange("p (h d) -> p h d", d=DH)
                    at = slice(k * NG * P, (k + 1) * NG * P)
                    dst = [wqk[:, l, part, at].rearrange("p (h r) -> p h r", r=ST) for part in range(2)]
                    for r in range(3):
                        rs = slice(r * DH, (r + 1) * DH)
                        split(dst[0][:, :, rs], dst[1][:, :, rs], w)
                split(wv[:, l, 0], wv[:, l, 1], src[:, 2])
                split(wo[:, l, 0], wo[:, l, 1], src[:, 3])
                split(wr[:, l, 0], wr[:, l, 1], rstage[:, l])
            split(b2s[:, 0], b2s[:, 1], b2st[:])
            v.wait_ge(s_sp, 4)
            link(vec.tensor_copy(flat(bvb[:]), U[:, 1, 0:2 * D]))
            link(vec.tensor_copy(flat(bob[:]), U[:, 1, 2 * D:4 * D]))
            link(vec.tensor_copy(lnwb[:], U[:, 2, 0:D]))
            link(vec.tensor_copy(lnbb[:], U[:, 2, D:2 * D]))
            link(vec.tensor_copy(bgb[:], U[:, 2, 2 * D:2 * D + E]))
            link(vec.tensor_copy(flat(qkb[:]), U[:, 3, 0:4 * NG]))
            link(vec.tensor_copy(lom[:], U[:, 3, 4 * NG:4 * NG + 2]))
            link(vec.tensor_copy(b1c[:], Y[:, 0, 0:E * CH["ffn1"]]))
            for k, (_, dst, c) in enumerate(big):
                v.wait_ge(s_hs, k + 1)
                vec.scalar_tensor_tensor(dst[:, 1, c:c + E * F0], stage[:, k % 2], WS, dst[:, 0, c:c + E * F0],
                                         ALU.mult, ALU.subtract).then_inc(s_los, 1)
            v.wait_ge(s_los, len(big))
            v.sem_inc(s_go, 1)
            v.wait_ge(s_go, SETUP_DONE)
            steps = [0]

            def bcast(ap, n_, axis=2):
                shape = list(ap.shape)
                return ap.unsqueeze(axis).broadcast_to(shape[:axis] + [n_] + shape[axis:])

            def normed(it, ps, g):
                o = ps[:].rearrange("p (s j r) -> p s j r", j=HG, r=ST)
                steps[0] += 1
                vec.reciprocal(rec[:], o[:, :, :, DH]).then_inc(s_dve, 1)
                v.wait_ge(s_dve, count(it, s_dve, steps[0]))
                vec.tensor_tensor(ao[:, :, g * HG:(g + 1) * HG], o[:, :, :, 0:DH], bcast(rec[:], DH, 3),
                                  ALU.mult).then_inc(s_ao, 1)

            def hook(it, n, pos):
                m = n + 1

                def step(ins):
                    steps[0] += 1
                    ins.then_inc(s_dve, 1)
                    v.wait_ge(s_dve, count(it, s_dve, steps[0]))

                def statistics(src, tiles):
                    for s in tiles:
                        ins = vec.bn_stats(st6[:, s], src[:, s])
                    return ins

                def moments():
                    vec.memset(ve[:], 0.0)
                    for s in range(NS):
                        ins = vec.bn_aggr(mv[:, s], st6[:, s])
                    step(ins)
                    vec.tensor_scalar(ve[:], mv[:, :, 1], LN_EPS, None, ALU.add).then_inc(s_var, 1)

                def normalise(dst, src):
                    for s in range(NS):
                        ins = vec.tensor_scalar(dst[:, s], src[:, s], mv[:, s, 0:1], rstd[:, s:s + 1],
                                                ALU.subtract, ALU.mult)
                    return ins

                b = n - 1
                if b >= 0 and is_ffn(b) and pos == 3:
                    v.wait_ge(s_fin, count(it, s_fin, b + 1))
                    if b < SLOTS:
                        v.wait_ge(s_out, it * 16 * SLOTS + 1)
                    vec.scalar_tensor_tensor(flat(xw[:, b % 2]), T1[:], 0.5 / WS, flat(xres(b)), ALU.mult,
                                             ALU.add).then_inc(s_x, 1)
                if b >= 0 and not is_ffn(b):
                    i, res = ai(b), xw[:, b % 2]
                    if pos == 1:
                        v.wait_ge(s_ot, count(it, s_ot, (i + 1) * NG))
                        normed(it, T1, NG - 1)
                    if pos == 3:
                        v.wait_ge(s_ah, count(it, s_ah, i + 1))
                        vec.tensor_tensor(aT[:, 1], T1[:], aT[:, 0], ALU.subtract).then_inc(s_al, 1)
                    if pos == 5:
                        v.wait_ge(s_rb, count(it, s_rb, i + 1))
                        v.wait_ge(s_fin, count(it, s_fin, b + 1))
                        vec.scalar_tensor_tensor(flat(res), T1[:], 1 / WS, flat(res), ALU.mult,
                                                 ALU.add).then_inc(s_x, 1)
                if m > MAINS:
                    return
                a = m % 2
                if hook_of(n, pos, "stats"):
                    if b >= 0:
                        v.wait_ge(s_x, count(it, s_x, b + 1))
                    if m % MAINS < SLOTS:
                        v.wait_ge(s_xin[a], (it + m // MAINS) * 16 + 16)
                    statistics(xres(m), range(NS // 2))
                if hook_of(n, pos, "moments"):
                    step(statistics(xres(m), range(NS // 2, NS)))
                    moments()
                if hook_of(n, pos, "norm"):
                    v.wait_ge(s_rstd, count(it, s_rstd, LNBASE[m] + 1))
                    if kind(m) != "full":
                        normalise(xn[:, a], xres(m)).then_inc(s_xn, 1)
                    else:
                        step(normalise(zz[:, a], xres(m)))
                        step(statistics(zz[:, a], range(NS)))
                        moments()
                if hook_of(n, pos, "norm2") and kind(m) == "full":
                    v.wait_ge(s_rstd, count(it, s_rstd, LNBASE[m] + 2))
                    normalise(xn[:, a], zz[:, a]).then_inc(s_n2, 1)
                if hook_of(n, pos, "xl"):
                    v.wait_ge(s_xh, count(it, s_xh, m + 1))
                    vec.tensor_tensor(xT[:, a, 1, PADL:PADL + T], T1[:], xT[:, a, 0, PADL:PADL + T],
                                      ALU.subtract).then_inc(s_xl, 1)
                if not is_ffn(m):
                    for p in range(2):
                        if hook_of(n, pos, "strip%d" % p):
                            strips(it, m, p)
                    return
                if hook_of(n, pos, "logits"):
                    v.wait_ge(s_lg, count(it, s_lg, fi(m) + 1))
                    logits = T1[:, 0:NS * E].rearrange("p (s e) -> p s e", e=E)
                    if kind(m) == "ffn0":
                        step(vec.tensor_scalar(lg[:], logits, 1 / WS, None, ALU.mult))
                    else:
                        step(vec.scalar_tensor_tensor(lg[:], logits, 1 / WS, bcast(bgb[:], NS, 1), ALU.mult,
                                                      ALU.add))
                    step(vec.tensor_reduce(mx[:], lg[:], AX, ALU.max))
                    vec.tensor_tensor(cw[:], lg[:], bcast(mx[:], E), ALU.subtract).then_inc(s_ls, 1)
                if hook_of(n, pos, "rank"):
                    other, own = bcast(lg[:], E, 2), bcast(lg[:], E, 3)
                    vec.tensor_tensor(gt[:], other, own, ALU.is_gt)
                    step(vec.tensor_tensor(eq[:], other, own, ALU.is_equal))
                    step(vec.tensor_tensor(eq[:], eq[:], bcast(tri[:], NS, 1), ALU.mult))
                    step(vec.tensor_tensor(gt[:], gt[:], eq[:], ALU.add))
                    vec.tensor_reduce(rank[:], gt[:], AX, ALU.add)
                if hook_of(n, pos, "weights"):
                    v.wait_ge(s_ex, count(it, s_ex, fi(m) + 1))
                    step(vec.tensor_scalar(cw[:], ex[:], -1.0, 1.0, ALU.mult, ALU.add))
                    step(vec.reciprocal(cw[:], cw[:]))
                    step(vec.scalar_tensor_tensor(flat(ex[:]), flat(ex[:]), 1.0, flat(cw[:]), ALU.add, ALU.mult))
                    step(vec.scalar_tensor_tensor(flat(cw[:]), flat(rank[:]), 1.5, flat(ex[:]), ALU.is_lt, ALU.mult))
                    step(vec.tensor_reduce(ssum[:], cw[:], AX, ALU.add))
                if hook_of(n, pos, "combine"):
                    if kind(m) == "ffn1":
                        step(vec.tensor_reduce(zs[:], ex[:], AX, ALU.add))
                        step(vec.scalar_tensor_tensor(ssum[:], zs[:], 1e-8, ssum[:], ALU.mult, ALU.add))
                    step(vec.reciprocal(ssum[:], ssum[:]))
                    step(vec.tensor_tensor(cw[:], cw[:], bcast(ssum[:], E), ALU.mult))
                    step(vec.tensor_copy(c2[:, :, 0:E], cw[:]))
                    vec.tensor_tensor(c2[:, :, E:2 * E], cw[:], c2[:, :, 0:E], ALU.subtract).then_inc(s_c2, 1)

            def strips(it, n, p):
                i, g = ai(n), p // 2
                hi_, exact, mask = qk16[:, p % 2], qk32[:, p % 2], lom[:, p % 2:p % 2 + 1]
                v.wait_ge(s_pb, count(it, s_pb, i * 2 * NG + p + 1))
                if p % 2 == 0:
                    vec.scalar_tensor_tensor(q3[:, g, 0:T], hi_, mask, exact, ALU.mult, ALU.add).then_inc(s_qs, 1)
                    return
                v.wait_ge(s_kz, count(it, s_kz, i * (NG - 1) + max(g - 2, 0)))
                vec.scalar_tensor_tensor(k3[:, g % 2], hi_, mask, exact, ALU.mult, ALU.add).then_inc(s_kt, 1)
                if g == 0:
                    v.wait_ge(s_kt, count(it, s_kt, i * NG + 1))
                    for j in range(HG):
                        ins = vec.tensor_scalar(kz[:, j, PADL:PADL + T], k3[:, 0], smask[:, j:j + 1], None, ALU.mult)
                    ins.then_inc(s_k0, 1)

            def beside_chunk(it, n, q):
                k, i = kind(n), fi(n)
                if k == "ffn1" and expert_at(n, q, LAG[k]["dve"]) is not None:
                    e = expert_at(n, q, LAG[k]["dve"])
                    v.wait_ge(s_cb, count(it, s_cb, i * E + e + 1))
                    vec.tensor_copy(cbs[:, e % 2], T0[:]).then_inc(s_cs, 1)
                if expert_at(n, q, LEAD[k] + 1) is not None:
                    e = expert_at(n, q, LEAD[k] + 1)
                    v.wait_ge(s_dn, count(it, s_dn, chunk(n, (e + 1) * CH[k])))
                    v.wait_ge(s_cs, count(it, s_cs, i * E + e + 1))
                    v.wait_ge(s_ac, count(it, s_ac, i * E + e - 1))
                    vec.tensor_tensor(yc[:, e % 2], Y[:, e % 2], cbs[:, e % 2], ALU.mult).then_inc(s_yc, 1)
                if behind(n, q, "dve") is not None:
                    hook(it, n, behind(n, q, "dve"))

            def ffn(it, n):
                k, i = kind(n), fi(n)
                L, nch = LEAD[k], E * CH[k]

                for q in range(nch):
                    Q = chunk(n, q)
                    if k == "ffn0":
                        v.wait_ge(s_si, count(it, s_si, glu(n, q) + 1))
                        v.wait_ge(s_up, count(it, s_up, Q + 1))
                        v.wait_ge(s_lo, count(it, s_lo, glu(n, q) - 3))
                        vec.scalar_tensor_tensor(gated[:, Q % 4], U[:, 2 * (q % 2) + 1], 1 / WS, act[:, q % 4],
                                                 ALU.mult, ALU.mult).then_inc(s_pr, 1)
                    else:
                        v.wait_ge(s_hf, count(it, s_hf, plain(n, q) + 1))
                        vec.tensor_tensor(lo[:, Q % 4], U[:, q % 4], hi[:, Q % 4], ALU.subtract).then_inc(s_l1, 1)
                    if follows(n) and q <= L:
                        beside_chunk(it, n - 1, E * CH[kind(n - 1)] + q)
                    if q == (2 if follows(n) else 1):
                        v.wait_ge(s_cp, count(it, s_cp, i + 1))
                        vec.tensor_copy(cT[:, n % 2], T1h[0:2 * E, 0:T]).then_inc(s_ct, 1)
                    beside_chunk(it, n, q)
                if not follows(n + 1):
                    for q in range(L + 1):
                        beside_chunk(it, n, nch + q)

            def attention(it, n):
                k, i = kind(n), ai(n)
                l = 0 if k == "win" else 1
                full = k == "full"
                nu = UNITS[k]
                nb, w, width = (NS, P, T) if full else (NB, QB, TP)

                def values_kept():
                    v.wait_ge(s_vp, count(it, s_vp, i + 1))
                    for b in range(nb):
                        src = Y[:, 0, b * P:(b + 1) * P] if full else Y[:, b // HB, (b % HB) * P:(b % HB + 1) * P]
                        ins = vec.scalar_tensor_tensor(v4[:, b, :, 0:DH], src.rearrange("p (h d) -> p h d", d=DH),
                                                       1 / WS, bvb[:, l].rearrange("p (h d) -> p h d", d=DH),
                                                       ALU.mult, ALU.add)
                    ins.then_inc(s_v, 1)

                def maxima(g, u):
                    v.wait_ge(s_sa, count(it, s_sa, unit(n, g, u) + 1))
                    t, j = u // HG, u % HG
                    if full:
                        vec.tensor_reduce(mxs[:, g % 2, j, t:t + 1], U[:, u % 2], AX, ALU.max).then_inc(s_mx, 1)
                    else:
                        vec.tensor_reduce(mxs[0:QB, g % 2, j, t * HB:(t + 1) * HB],
                                          U[0:QB, u % 2, 0:HB * P].rearrange("p (b k) -> p b k", k=P), AX,
                                          ALU.max).then_inc(s_mx, 1)

                def negate(g):
                    v.wait_ge(s_mx, count(it, s_mx, unit(n, g, nu)))
                    dst = mp[0:w, g % 2, 0:nb].rearrange("p b (j r) -> p b j r", r=ST)[:, :, :, MROW]
                    vec.tensor_scalar(dst, mxs[0:w, g % 2, :, 0:nb].rearrange("p j b -> p b j"), -1.0, None,
                                      ALU.mult).then_inc(s_mp, 1)

                def with_max(g):
                    v.wait_ge(s_mt, count(it, s_mt, i * NG + g + 1))
                    vec.tensor_tensor(q3m[:, g % 2, 0:width], T0h[:, 0:width], q3[:, g, 0:width], ALU.add)\
                        .then_inc(s_qm, 1)

                for u in range(nu + 2):
                    if u < nu:
                        maxima(0, u)
                    for what in beside(n, u - 2):
                        if what == "V":
                            values_kept()
                        elif type(what) is tuple:
                            hook(it, n, what[1])
                        elif what < 2 * NG - 2:
                            strips(it, n, what)
                negate(0)
                maxima(1, 0)
                with_max(0)
                maxima(1, 1)
                strips(it, n, 2 * NG - 2)
                strips(it, n, 2 * NG - 1)
                hook(it, n, 2)
                for g in range(NG):
                    for u in range(nu):
                        if g + 1 + (u + AHEAD) // nu < NG:
                            maxima(g + 1 + (u + AHEAD) // nu, (u + AHEAD) % nu)
                        if u == nu - 1 - AHEAD and g + 1 < NG:
                            negate(g + 1)
                        if u == nu - AHEAD and g + 1 < NG:
                            with_max(g + 1)
                        if u == nu // 2 + 1 and g:
                            v.wait_ge(s_ot, count(it, s_ot, i * NG + g))
                            normed(it, T0, g - 1)
                        if within(n, g, u) is not None:
                            hook(it, n, within(n, g, u))

            for pos in range(POS):
                hook(0, -1, pos)
            before = steps[0]
            with v.Fori(0, BODIES) as it:
                for n in range(MAINS):
                    (ffn if is_ffn(n) else attention)(it, n)
                hook(it, MAINS, 3)
            assert steps[0] - before == DVE_STEPS, steps[0] - before


_INS = ['L0_attn_x', 'L0_attn_Wq', 'L0_attn_bq', 'L0_attn_Wk', 'L0_attn_bk', 'L0_attn_Wv', 'L0_attn_bv',
        'L0_attn_Wo', 'L0_attn_bo', 'L0_ffn_router_w', 'L0_ffn_w1', 'L0_ffn_w3', 'L0_ffn_w2',
        'L1_attn_ln_w', 'L1_attn_ln_b', 'L1_attn_W_qkv', 'L1_attn_b_qkv', 'L1_attn_W_proj',
        'L1_attn_b_proj', 'L1_ffn_Wg', 'L1_ffn_bg', 'L1_ffn_W1', 'L1_ffn_b1', 'L1_ffn_W2', 'L1_ffn_b2']


def kernel(**inputs):
    import numpy as _np
    import concourse.bacc as _bacc
    from concourse import mybir as _mybir
    from concourse.bass_utils import run_bass_kernel_spmd as _run

    nc = _bacc.Bacc("TRN2", target_bir_lowering=False, num_devices=1)
    arrays, args = {}, []
    for name in _INS:
        a = _np.ascontiguousarray(inputs[name])
        arrays[f"in_{name}_dram"] = a
        args.append(nc.dram_tensor(f"in_{name}_dram", a.shape, _mybir.dt.from_np(a.dtype), kind="ExternalInput").ap())
    shape = arrays["in_L0_attn_x_dram"].shape
    args.append(nc.dram_tensor("out_0_dram", shape, _mybir.dt.float32, kind="ExternalOutput").ap())
    build(nc, *args)
    r = _run(nc, [arrays], core_ids=[0])
    return r.results[0]["out_0_dram"]
```
